# Optimizing a Trainium2 kernel written in Bass

```python
import numpy as np
import jax
import jax.numpy as jnp

def _softmax(x, axis=-1):
    return jax.nn.softmax(x, axis=axis)

def _gelu(x):
    return jax.nn.gelu(x, approximate=True)

def _silu(x):
    return jax.nn.silu(x)

def _sigmoid(x):
    return jax.nn.sigmoid(x)

def _layernorm(x, axis=-1, eps=1e-05):
    m = jnp.mean(x, axis=axis, keepdims=True)
    v = jnp.var(x, axis=axis, keepdims=True)
    return (x - m) / jnp.sqrt(v + eps)

def _scatter_add(tgt, idx, src, axis=0):
    return tgt.at[idx].add(src)

def _segment_sum(src, seg, n):
    return jax.ops.segment_sum(src, seg, n)
kernel_name = 'mk_conv_seq_d2_conv_nchw96_r2_13c71b'

def setup_inputs(seed: int=0):
    np.random.seed(seed)
    _w = jnp.asarray

    def _rec_inputs():
        import jax
        import jax.numpy as jnp
        _gk = jax.random.key(seed)
        x = -0.0001538 + 1 * jax.random.normal(jax.random.fold_in(_gk, 1), (16, 48, 32, 32), jnp.float32)
        return x
    x = _rec_inputs()

    def _L0_conv_setup():
        import jax, jax.numpy as jnp
        import numpy as np
        WS = 8
        K = 9
        BN_EPS = 1e-05

        def conv1x1(x, w, b):
            return jnp.einsum('bchw,oc->bohw', x, w) + b[None, :, None, None]

        def affine(x, s, t):
            return x * s[None, :, None, None] + t[None, :, None, None]

        def window_partition(x, ws):
            B, C, H, W = x.shape
            x = x.reshape(B, C, H // ws, ws, W // ws, ws)
            x = x.transpose(0, 2, 4, 1, 3, 5)
            return x.reshape(-1, C, ws, ws)

        def window_reverse(win, ws, B, H, W):
            C = win.shape[1]
            x = win.reshape(B, H // ws, W // ws, C, ws, ws)
            x = x.transpose(0, 3, 1, 4, 2, 5)
            return x.reshape(B, C, H, W)

        def knn_idx(nodes, k):
            nrm = jnp.maximum(jnp.linalg.norm(nodes, axis=-1, keepdims=True), 1e-12)
            xn = nodes / nrm
            sq = jnp.sum(xn * xn, axis=-1, keepdims=True)
            dist = sq - 2.0 * jnp.einsum('bnc,bmc->bnm', xn, xn) + sq.transpose(0, 2, 1)
            _, idx = jax.lax.top_k(-dist, k)
            return idx
        key = jax.random.key(seed)
        ks = jax.random.split(key, 16)
        B, C, H, W = (16, 48, 32, 32)
        O = 2 * C

        def bn(k1, k2, n):
            g = 1.0 + 0.1 * jax.random.normal(k1, (n,), jnp.float32)
            b = 0.1 * jax.random.normal(k2, (n,), jnp.float32)
            return (g, b)
        x = jax.random.normal(ks[0], (B, C, H, W), jnp.float32)
        fc1_w = 0.05 * jax.random.normal(ks[1], (C, C), jnp.float32)
        fc1_b = 0.02 * jax.random.normal(ks[2], (C,), jnp.float32)
        fc1_s, fc1_t = bn(ks[3], ks[4], C)
        ew = 0.05 * jax.random.normal(ks[5], (O, 2 * C), jnp.float32)
        eb = 0.02 * jax.random.normal(ks[6], (O,), jnp.float32)
        es, et = bn(ks[7], ks[8], O)
        fc2_w = 0.05 * jax.random.normal(ks[9], (C, O), jnp.float32)
        fc2_b = 0.02 * jax.random.normal(ks[10], (C,), jnp.float32)
        fc2_s, fc2_t = bn(ks[11], ks[12], C)
        return {'x': x, 'fc1_w': fc1_w, 'fc1_b': fc1_b, 'fc1_s': fc1_s, 'fc1_t': fc1_t, 'ew': ew, 'eb': eb, 'es': es, 'et': et, 'fc2_w': fc2_w, 'fc2_b': fc2_b, 'fc2_s': fc2_s, 'fc2_t': fc2_t}
    _L0_conv_all = _L0_conv_setup()
    _L0_conv_in = {k: v for k, v in _L0_conv_all.items() if k in ('fc1_w', 'fc1_b', 'fc1_s', 'fc1_t', 'ew', 'eb', 'es', 'et', 'fc2_w', 'fc2_b', 'fc2_s', 'fc2_t')}
    del _L0_conv_all

    def _L1_conv_setup():
        import jax, jax.numpy as jnp
        import numpy as np
        from jax import lax
        B, C, H, W = (8, 48, 96, 96)
        HC = 48
        EPS = 1e-05

        def _convlstm_scan(x_rows, w_mid, b, reverse):
            hc = w_mid.shape[0] // 4
            dn = ('NCH', 'OIH', 'NCH')

            def step(carry, xr):
                h, c = carry
                inp = jnp.concatenate([xr, h], axis=1)
                gates = lax.conv_general_dilated(inp, w_mid, (1,), 'SAME', dimension_numbers=dn) + b[None, :, None]
                i, f, g, o = jnp.split(gates, 4, axis=1)
                c2 = jax.nn.sigmoid(f) * c + jax.nn.sigmoid(i) * jnp.tanh(g)
                h2 = jax.nn.sigmoid(o) * jnp.tanh(c2)
                return ((h2, c2), h2)
            z = jnp.zeros((x_rows.shape[1], hc, x_rows.shape[3]), x_rows.dtype)
            _, hs = lax.scan(step, (z, z), x_rows, reverse=reverse)
            return hs
        key = jax.random.key(seed)
        ks = jax.random.split(key, 6)
        s = 0.05
        x = jax.random.normal(ks[0], (B, C, H, W), jnp.float32)
        w_f = jax.random.normal(ks[1], (4 * HC, C + HC, 3, 3), jnp.float32) * s
        b_f = jnp.zeros((4 * HC,), jnp.float32)
        w_b = jax.random.normal(ks[2], (4 * HC, C + HC, 3, 3), jnp.float32) * s
        b_b = jnp.zeros((4 * HC,), jnp.float32)
        w_proj = jax.random.normal(ks[3], (C, 2 * HC), jnp.float32) * s
        gamma = jnp.ones((C,), jnp.float32)
        beta = jnp.zeros((C,), jnp.float32)
        return {'x': x, 'w_f': w_f, 'b_f': b_f, 'w_b': w_b, 'b_b': b_b, 'w_proj': w_proj, 'gamma': gamma, 'beta': beta}
    _L1_conv_all = _L1_conv_setup()
    _L1_conv_in = {k: v for k, v in _L1_conv_all.items() if k in ('w_f', 'b_f', 'w_b', 'b_b', 'w_proj', 'gamma', 'beta')}
    del _L1_conv_all
    return {'x': x, 'L0_conv_fc1_w': _L0_conv_in['fc1_w'], 'L0_conv_fc1_b': _L0_conv_in['fc1_b'], 'L0_conv_fc1_s': _L0_conv_in['fc1_s'], 'L0_conv_fc1_t': _L0_conv_in['fc1_t'], 'L0_conv_ew': _L0_conv_in['ew'], 'L0_conv_eb': _L0_conv_in['eb'], 'L0_conv_es': _L0_conv_in['es'], 'L0_conv_et': _L0_conv_in['et'], 'L0_conv_fc2_w': _L0_conv_in['fc2_w'], 'L0_conv_fc2_b': _L0_conv_in['fc2_b'], 'L0_conv_fc2_s': _L0_conv_in['fc2_s'], 'L0_conv_fc2_t': _L0_conv_in['fc2_t'], 'L1_conv_w_f': _L1_conv_in['w_f'], 'L1_conv_b_f': _L1_conv_in['b_f'], 'L1_conv_w_b': _L1_conv_in['w_b'], 'L1_conv_b_b': _L1_conv_in['b_b'], 'L1_conv_w_proj': _L1_conv_in['w_proj'], 'L1_conv_gamma': _L1_conv_in['gamma'], 'L1_conv_beta': _L1_conv_in['beta']}

def reference(x, L0_conv_fc1_w, L0_conv_fc1_b, L0_conv_fc1_s, L0_conv_fc1_t, L0_conv_ew, L0_conv_eb, L0_conv_es, L0_conv_et, L0_conv_fc2_w, L0_conv_fc2_b, L0_conv_fc2_s, L0_conv_fc2_t, L1_conv_w_f, L1_conv_b_f, L1_conv_w_b, L1_conv_b_b, L1_conv_w_proj, L1_conv_gamma, L1_conv_beta):
    import jax
    import jax.numpy as jnp

    def _L0_conv_ref(x, fc1_w, fc1_b, fc1_s, fc1_t, ew, eb, es, et, fc2_w, fc2_b, fc2_s, fc2_t):
        import jax, jax.numpy as jnp
        import numpy as np
        WS = 8
        K = 9
        BN_EPS = 1e-05

        def conv1x1(x, w, b):
            return jnp.einsum('bchw,oc->bohw', x, w) + b[None, :, None, None]

        def affine(x, s, t):
            return x * s[None, :, None, None] + t[None, :, None, None]

        def window_partition(x, ws):
            B, C, H, W = x.shape
            x = x.reshape(B, C, H // ws, ws, W // ws, ws)
            x = x.transpose(0, 2, 4, 1, 3, 5)
            return x.reshape(-1, C, ws, ws)

        def window_reverse(win, ws, B, H, W):
            C = win.shape[1]
            x = win.reshape(B, H // ws, W // ws, C, ws, ws)
            x = x.transpose(0, 3, 1, 4, 2, 5)
            return x.reshape(B, C, H, W)

        def knn_idx(nodes, k):
            nrm = jnp.maximum(jnp.linalg.norm(nodes, axis=-1, keepdims=True), 1e-12)
            xn = nodes / nrm
            sq = jnp.sum(xn * xn, axis=-1, keepdims=True)
            dist = sq - 2.0 * jnp.einsum('bnc,bmc->bnm', xn, xn) + sq.transpose(0, 2, 1)
            _, idx = jax.lax.top_k(-dist, k)
            return idx
        B, C, H, W = x.shape
        tmp = x
        y = affine(conv1x1(x, fc1_w, fc1_b), fc1_s, fc1_t)
        win = window_partition(y, WS)
        Bw = win.shape[0]
        nodes = win.reshape(Bw, C, WS * WS).transpose(0, 2, 1)
        idx = jax.lax.stop_gradient(knn_idx(nodes, K))
        x_j = jax.vmap(lambda n, i: n[i])(nodes, idx)
        x_i = nodes[:, :, None, :]
        feat = jnp.concatenate([jnp.broadcast_to(x_i, x_j.shape), x_j - x_i], axis=-1)
        h = jnp.einsum('bnkc,oc->bnko', feat, ew) + eb
        h = h * es + et
        h = jax.nn.gelu(h, approximate=False)
        h = jnp.max(h, axis=2)
        O = h.shape[-1]
        win_out = h.transpose(0, 2, 1).reshape(Bw, O, WS, WS)
        y = window_reverse(win_out, WS, B, H, W)
        y = affine(conv1x1(y, fc2_w, fc2_b), fc2_s, fc2_t)
        return y + tmp

    def _L1_conv_ref(x, w_f, b_f, w_b, b_b, w_proj, gamma, beta):
        import jax, jax.numpy as jnp
        import numpy as np
        from jax import lax
        B, C, H, W = (8, 48, 96, 96)
        HC = 48
        EPS = 1e-05

        def _convlstm_scan(x_rows, w_mid, b, reverse):
            hc = w_mid.shape[0] // 4
            dn = ('NCH', 'OIH', 'NCH')

            def step(carry, xr):
                h, c = carry
                inp = jnp.concatenate([xr, h], axis=1)
                gates = lax.conv_general_dilated(inp, w_mid, (1,), 'SAME', dimension_numbers=dn) + b[None, :, None]
                i, f, g, o = jnp.split(gates, 4, axis=1)
                c2 = jax.nn.sigmoid(f) * c + jax.nn.sigmoid(i) * jnp.tanh(g)
                h2 = jax.nn.sigmoid(o) * jnp.tanh(c2)
                return ((h2, c2), h2)
            z = jnp.zeros((x_rows.shape[1], hc, x_rows.shape[3]), x_rows.dtype)
            _, hs = lax.scan(step, (z, z), x_rows, reverse=reverse)
            return hs
        xr = jnp.transpose(x, (2, 0, 1, 3))
        hs_f = _convlstm_scan(xr, w_f[:, :, 1, :], b_f, reverse=False)
        hs_b = _convlstm_scan(xr, w_b[:, :, 1, :], b_b, reverse=True)
        feats = jnp.concatenate([hs_f, hs_b], axis=2)
        feats = jnp.transpose(feats, (1, 2, 0, 3))
        y = jnp.einsum('oc,bchw->bohw', w_proj, feats)
        mu = jnp.mean(y, axis=(0, 2, 3))
        var = jnp.var(y, axis=(0, 2, 3))
        yn = (y - mu[None, :, None, None]) * lax.rsqrt(var + EPS)[None, :, None, None]
        y = gamma[None, :, None, None] * yn + beta[None, :, None, None]
        return jax.nn.relu(y) + x

    def _gn(v, G=32, eps=1e-05):
        B_, C_, H_, W_ = v.shape
        g = v.reshape(B_, G, C_ // G, H_, W_)
        m = jnp.mean(g, axis=(2, 3, 4), keepdims=True)
        s = jnp.var(g, axis=(2, 3, 4), keepdims=True)
        return ((g - m) / jnp.sqrt(s + eps)).reshape(v.shape)

    def _ln_c(v, eps=1e-06):
        m = jnp.mean(v, axis=1, keepdims=True)
        s = jnp.var(v, axis=1, keepdims=True)
        return (v - m) / jnp.sqrt(s + eps)

    def _ln_t(v, eps=1e-05):
        m = jnp.mean(v, axis=-1, keepdims=True)
        s = jnp.var(v, axis=-1, keepdims=True)
        return (v - m) / jnp.sqrt(s + eps)

    def _to_tokens(v):
        B_, C_, H_, W_ = v.shape
        return v.reshape(B_, C_, H_ * W_).transpose(0, 2, 1)

    def _from_tokens(t, like):
        B_, C_, H_, W_ = like.shape
        return t.transpose(0, 2, 1).reshape(B_, C_, H_, W_)
    x = _L0_conv_ref(x, L0_conv_fc1_w, L0_conv_fc1_b, L0_conv_fc1_s, L0_conv_fc1_t, L0_conv_ew, L0_conv_eb, L0_conv_es, L0_conv_et, L0_conv_fc2_w, L0_conv_fc2_b, L0_conv_fc2_s, L0_conv_fc2_t)
    x = _L1_conv_ref(x, L1_conv_w_f, L1_conv_b_f, L1_conv_w_b, L1_conv_b_b, L1_conv_w_proj, L1_conv_gamma, L1_conv_beta)
    return x

_drawn_inputs = setup_inputs


def setup_inputs(seed=0):
    import zlib

    import numpy as np

    out = dict(_drawn_inputs(seed))
    spreads = {'L1_conv_b_f': (0.0, 2.0),
     'L1_conv_b_b': (0.0, 2.0),
     'L1_conv_gamma': (1.0, 0.6),
     'L1_conv_beta': (0.0, 2.0)}
    factors = {'L0_conv_fc1_b': 8.0,
     'L0_conv_fc1_s': 4.365,
     'L0_conv_fc1_t': 4.072,
     'L0_conv_eb': 8.0,
     'L0_conv_es': 7.466,
     'L0_conv_fc2_b': 9.407,
     'L0_conv_fc2_s': 7.416,
     'L0_conv_et': 4.047,
     'L0_conv_fc2_t': 8.0,
     'L1_conv_w_f': 3.517,
     'L1_conv_w_b': 3.298}
    for name, (base, spread) in spreads.items():
        noise = np.random.default_rng([zlib.crc32(name.encode()), seed]).standard_normal(out[name].shape)
        drawn = base * np.exp(spread * noise) if base else spread * noise
        out[name] = jnp.asarray(drawn.astype(out[name].dtype))
    for name, factor in factors.items():
        out[name] = (out[name] * factor).astype(out[name].dtype)
    return out
```

```python
from contextlib import ExitStack

import concourse.bass as bass
from concourse import mybir

F32 = mybir.dt.float32
F32R = mybir.dt.float32r
U16 = mybir.dt.uint16
ALU = mybir.AluOpType
ACT = mybir.ActivationFunctionType
AX_X = mybir.AxisListType.X

P = 128
B, C, H, W = 16, 48, 32, 32
O = 2 * C
WS = 8
NODES = WS * WS
K = 9
PAIRS = B // 2
WROWS = H // WS
GROUPS = WROWS * PAIRS
WIN = 2 * (W // WS)
GN = WIN * NODES
HG = GN // 2
CHUNK = 512
CHUNKS = GROUPS * HG // CHUNK
HALF = 64
TOP = HALF + C
E9 = NODES * K
SLOT = (W + 1) * B + 2
TAPS = 3
BX = B // 2
NX = BX * W
EPS = 1e-5
LOWEST = -3.0e38


def split(t):
    return t.rearrange("p (h n) -> p h n", h=2)


def build(nc, xs, xrow, w1, ones_sel, col1, jcol, wedge, edge_scale, edge_shift, ident9, w2, col2,
          wl, wp, gb, comb, out):
    yf_d = nc.dram_tensor("yf_d", [C, GROUPS, 2, HG], F32, kind="Internal").ap()
    yhi_d = nc.dram_tensor("yhi_d", [C, GROUPS, 2, HG], F32, kind="Internal").ap()
    ylo_d = nc.dram_tensor("ylo_d", [C, GROUPS, 2, HG], F32, kind="Internal").ap()
    nr_d = nc.dram_tensor("nr_d", [3, CHUNKS, 2, 2, HG], F32, kind="Internal").ap()
    idx_d = nc.dram_tensor("idx_d", [GROUPS, WIN, NODES, K], U16, kind="Internal").ap()
    x1_d = nc.dram_tensor("x1_d", [H, C, B, W], F32, kind="Internal").ap()
    hist_d = nc.dram_tensor("hist_d", [H, 2, C, B, W], F32, kind="Internal").ap()

    with ExitStack() as ctx:
        def sem(name):
            return ctx.enter_context(nc.semaphore(name))

        def sb_in(stack):
            return lambda name, shape, dt: stack.enter_context(nc.sbuf_tensor(name, shape, dt))

        sb = sb_in(ctx)
        xh_hi = sb("xh_hi", [P, H, SLOT], F32R)
        xh_lo = sb("xh_lo", [P, H, SLOT], F32R)

        with ExitStack() as s0:
            a = sb_in(s0)
            x_in = a("x_in", [P, 2, CHUNK], F32)
            w1_sb = a("w1_sb", [P, P], F32)
            sel_sb = a("sel_sb", [P, CHUNKS, 2 * CHUNKS], F32)
            col1_sb = a("col1_sb", [P, 3], F32)
            t1 = a("t1", [P, 2], F32)
            y0 = a("y0", [P, 2, CHUNK], F32)
            y0_hi = a("y0_hi", [P, 2, CHUNK], F32R)
            y0_lo = a("y0_lo", [P, 2, CHUNK], F32R)
            y0_sq = a("y0_sq", [P, 2, CHUNK], F32)
            nrm = a("nrm", [2 * CHUNKS, CHUNK], F32)
            nmax = a("nmax", [2 * CHUNKS, CHUNK], F32)
            nunit = a("nunit", [2 * CHUNKS, CHUNK], F32)
            nrows = a("nrows", [2 * CHUNKS, 3, CHUNK], F32)

        with ExitStack() as s1:
            a = sb_in(s1)
            y_hl = a("y_hl", [P, 2, GN], F32R)
            xl = a("xl", [P, 2, GN], F32)
            xr = a("xr", [P, 2, GN], F32)
            side = a("side", [P, 2, GN], F32)
            ib = a("ib", [P, WIN, E9], U16)
            keys2 = a("keys2", [P, 2, NODES], F32)
            val8 = a("val8", [P, 2, 16], F32)
            idx = a("idx", [P, 2, 4, 16], U16)
            onehot = a("onehot", [P, 2, 2, E9], F32R)
            gel = a("gel", [O, 2, 2, E9], F32)
            hmax = a("hmax", [O, 2, GN], F32)
            ab = a("ab", [P, WIN, O], F32)
            ab_hi = a("ab_hi", [P, 2, WIN, O], F32R)
            ab_lo = a("ab_lo", [P, 2, WIN, O], F32R)
            jcol_sb = a("jcol_sb", [P, 1], F32)
            we_raw = a("we_raw", [P, 2, O], F32)
            we_mul = a("we_mul", [P, O], F32)
            we_add = a("we_add", [P, 2, O], F32)
            we = a("we", [P, 2, O], F32)
            we_hi = a("we_hi", [P, 2, O], F32R)
            we_lo = a("we_lo", [P, 2, O], F32R)
            w2_sb = a("w2_sb", [O, C], F32)
            col2_sb = a("col2_sb", [P, 3], F32)
            t2 = a("t2", [P, 2], F32)
            z2 = a("z2", [P, GN], F32)
            x1 = a("x1", [P, 2, GN], F32)

        with ExitStack() as s2:
            a = sb_in(s2)
            wl_raw = a("wl_raw", [P, 2, 2, TAPS, TOP], F32)
            wl_hi = a("wl_hi", [P, 2, 2, TAPS, TOP], F32R)
            wl_lo = a("wl_lo", [P, 2, 2, TAPS, TOP], F32R)
            ti = a("ti", [P, 2, NX], F32)
            tf = a("tf", [P, 2, NX], F32)
            tg = a("tg", [P, 2, NX], F32)
            to = a("to", [P, 2, NX], F32)
            cu = a("cu", [P, 2, NX], F32)
            cv = a("cv", [P, 2, NX], F32)
            c2 = a("c2", [P, 2, NX], F32)
            tc = a("tc", [P, 2, NX], F32)
            h2 = a("h2", [C, 2, 2, NX], F32)

        with ExitStack() as s3:
            a = sb_in(s3)
            wp_sb = a("wp_sb", [O, HALF], F32)
            gb_sb = a("gb_sb", [P, 2], F32)
            comb_sb = a("comb_sb", [P, 2, P], F32)
            hp = a("hp", [O, 2, 2, B * W], F32)
            y_sb = a("y_sb", [P, H // 2, B * W], F32)
            bst = a("bst", [P, H // 2, 6], F32)
            mv = a("mv", [P, 2], F32)
            st = a("st", [P, 8], F32)
            x1r = a("x1r", [P, 2, B * W], F32)
            act_y = a("act_y", [P, 2, B * W], F32)
            fin = a("fin", [P, 2, B * W], F32)

        pz = ctx.enter_context(nc.psum_tensor("pz", [P, 4, 512], F32))
        ps = [ctx.enter_context(nc.psum_tensor(f"ps{i}", [P, 512], F32)) for i in range(4)]
        p_fc1 = ps[0:2]
        p_nrm = ps[2]
        p_keys = ps[0]
        p_ab = ps[1:3]
        p_fc2 = ps[3]
        p_comb = ps[2]

        names = """pool_passed dve_passed consts0 x_in0 x_in1 fc1_done y_ready y_sq_ready nrm_done y_hi_ready y_split
            y_stored0 y_stored1 nrm_ready norm_parts nrows_ready nrows_stored t1_ready zeros_set
            consts1 edge_parts edge_w y_loaded0 y_loaded1 x_loaded0 x_loaded1 xres_loaded0 xres_loaded1
            ab_mm ab_copied ab_hi_ready ab_split xn_ready keys_done topk_done topk_parts idx_stored0
            idx_stored1 idx_here0 idx_here1 onehots z_done gelus maxed fc2_done z2_ready x1_ready
            x1_stored0 x1_stored1 x1_sum x1_hi own_set
            wl_loaded wl_scaled wl_split scan_init gates tanhs cells cell_parts tanh_c h2_ready h_hi
            h_lo hist0 hist1
            consts2 wp_ready hp_loaded0 hp_loaded1 y_mm y_kept y_stats fold comb_mm stat x1r0 x1r1
            relus summed out0 out1""".split()
        S = {n: sem(n) for n in names}
        block = ctx.enter_context(nc.Block())

        def reg(v, lo, n):
            return slice(v + lo, v + lo + n) if isinstance(v, int) else bass.ds(v + lo, n)

        def later(v, n=1):
            return not isinstance(v, int) or v >= n

        def passed(engine, name):
            engine.sem_inc(S[name], 1)

        def one_row(t, i):
            return t[:, reg(i, 0, 1)].rearrange("p o n -> p (o n)")

        def h_rows(t, row, x):
            at = (W + 1) * BX * x + 1
            return t[0:C, reg(row, 0, 1), at:at + (W + 1) * BX] \
                .rearrange("p o (b w) -> p (o b) w", w=W + 1)[:, :, 0:W]

        @block.sync
        def _(sp):
            sp.dma_start(w1_sb[:], w1).then_inc(S["consts0"], 16)
            sp.dma_start(sel_sb[:], ones_sel).then_inc(S["consts0"], 16)
            sp.dma_start(col1_sb[:], col1).then_inc(S["consts0"], 16)

            def load_x(c, b):
                sp.dma_start(x_in[:, b], xs[:, reg(c, 0, 1)].rearrange("p o n -> p (o n)")) \
                    .then_inc(S[f"x_in{b}"], 16)

            def store_y(c, b, src, dst):
                for h in range(2):
                    sp.dma_start(dst[:, reg(c * 2, 0, 2), h],
                                 split(src[HALF * h:HALF * h + C, b].bitcast(F32))).then_inc(S[f"y_stored{b}"], 16)

            load_x(0, 0)
            load_x(1, 1)
            with sp.Fori(0, CHUNKS // 2 - 1) as j:
                for b in range(2):
                    sp.wait_ge(S["y_split"], j * 2 + b + 1)
                    store_y(j * 2 + b, b, y0, yf_d)
                    store_y(j * 2 + b, b, y0_hi, yhi_d)
                    store_y(j * 2 + b, b, y0_lo, ylo_d)
                    sp.wait_ge(S["fc1_done"], j * 2 + b + 1)
                    load_x(j * 2 + 2 + b, b)
            for b in range(2):
                c = CHUNKS - 2 + b
                sp.wait_ge(S["y_split"], c + 1)
                store_y(c, b, y0, yf_d)
                store_y(c, b, y0_hi, yhi_d)
                store_y(c, b, y0_lo, ylo_d)
            sp.wait_ge(S["nrows_ready"], 3)
            for q in range(3):
                sp.dma_start(nr_d[q].rearrange("c h g n -> (c h) (g n)"), nrows[:, q]) \
                    .then_inc(S["nrows_stored"], 16)
            sp.wait_ge(S["nrows_stored"], 48)
            for b in range(2):
                sp.wait_ge(S[f"y_stored{b}"], 6 * 16 * CHUNKS // 2)

            sp.dma_start(jcol_sb[:], jcol).then_inc(S["consts1"], 16)
            sp.dma_start(we_raw[:], wedge).then_inc(S["consts1"], 16)
            sp.dma_start(we_mul[:], edge_scale.rearrange("(o n) -> o n", o=1).to_broadcast([P, O])) \
                .then_inc(S["consts1"], 16)
            sp.dma_start(we_add[:], edge_shift).then_inc(S["consts1"], 16)
            sp.dma_start(w2_sb[:], w2).then_inc(S["consts1"], 16)
            sp.dma_start(col2_sb[:], col2).then_inc(S["consts1"], 16)
            sp.dma_start(ab[HALF:P].rearrange("p w n -> p (w n)")[:, 0:E9], ident9).then_inc(S["consts1"], 16)

            sp.wait_ge(S["own_set"], 4)

            def load_group(g, b, par):
                for src, at in ((yhi_d, 0), (ylo_d, HALF)):
                    sp.dma_start(y_hl[at:at + C, b].bitcast(F32), src[:, reg(g, 0, 1)].rearrange("c o h n -> c (o h n)")) \
                        .then_inc(S[f"y_loaded{b}"], 16)
                sp.dma_start(xl[0:C, b], yf_d[:, reg(g, 0, 1)].rearrange("c o h n -> c (o h n)")) \
                    .then_inc(S[f"x_loaded{b}"], 16)
                for q, dst in ((0, side[0:C, b]), (1, xl[HALF:HALF + 1, b]), (2, xr[HALF:HALF + 1, b])):
                    src = nr_d[q, reg(par, 0, 1), :, b]
                    if q == 0:
                        src = src.to_broadcast([C, 2, HG])
                    sp.dma_start(split(dst), src).then_inc(S[f"x_loaded{b}"], 16)

            def load_xres(g, b):
                sp.dma_start(side[HALF:TOP, b], xrow[:, reg(g, 0, 1)].rearrange("c o n -> c (o n)")) \
                    .then_inc(S[f"xres_loaded{b}"], 16)

            def pass_idx(g, b, n):
                sp.wait_ge(S["topk_done"], g + 1)
                sp.dma_start(idx_d[reg(g, 0, 1)].rearrange("o (t s) n k -> (o s n) t k", s=2),
                             idx[:, b, :, 0:K]).then_inc(S[f"idx_stored{b}"], 16)
                sp.wait_ge(S[f"idx_stored{b}"], n * 16 + 16)
                sp.dma_start(ib[HALF * b:HALF * b + HALF],
                             idx_d[reg(g, 0, 1)].rearrange("o w n k -> o w (n k)")
                             .to_broadcast([HALF, WIN, E9])).then_inc(S[f"idx_here{b}"], 16)

            def store_x1(g, b):
                sp.wait_ge(S["x1_ready"], g + 1)
                wr = g // PAIRS
                p = g % PAIRS
                for h in range(2):
                    dst = x1_d[reg(wr * WS, 0, WS), :, reg(p, h * PAIRS, 1)]
                    sp.dma_start(dst.rearrange("r c o w -> c (r o) w"),
                                 x1[HALF:TOP, b].rearrange("c (h r w) -> c h r w", h=2, w=W)[:, h]) \
                        .then_inc(S[f"x1_stored{b}"], 16)

            load_group(0, 0, 0)
            load_group(1, 1, 0)
            load_xres(0, 0)
            load_xres(1, 1)
            pass_idx(0, 0, 0)

            def turn(g, b, j, last=False):
                if not (last and b):
                    pass_idx(g + 1, 1 - b, j + b)
                if not last:
                    sp.wait_ge(S["ab_mm"], g * 2 + 2)
                    sp.wait_ge(S["keys_done"], g + 1)
                    sp.wait_ge(S["topk_done"], g + 1)
                    load_group(g + 2, b, j + 1)
                store_x1(g, b)
                if not last:
                    load_xres(g + 2, b)

            with sp.Fori(0, GROUPS // 2 - 1) as j:
                for b in range(2):
                    turn(j * 2 + b, b, j)
            for b in range(2):
                turn(GROUPS - 2 + b, b, GROUPS // 2 - 1, last=True)
            for b in range(2):
                sp.wait_ge(S[f"x1_stored{b}"], 32 * (GROUPS // 2))

            sp.dma_start(wl_raw[:], wl).then_inc(S["wl_loaded"], 16)

            def store_h(s, x):
                sp.wait_ge(S["h2_ready"], s * 4 + (2 * x + 2))
                for d, row in ((0, s), (1, s * -1 + (H - 1))):
                    dst = hist_d[reg(row, 0, 1), d, :, BX * x:BX * x + BX].rearrange("o c b w -> (o c) (b w)")
                    sp.dma_start(dst, h2[:, x, d]).then_inc(S[f"hist{x}"], 16)

            with sp.Fori(0, H) as s:
                for x in range(2):
                    store_h(s, x)
            for x in range(2):
                sp.wait_ge(S[f"hist{x}"], 32 * H)

            sp.dma_start(wp_sb[:], wp).then_inc(S["consts2"], 16)
            sp.dma_start(gb_sb[:], gb).then_inc(S["consts2"], 16)
            sp.dma_start(comb_sb[:], comb).then_inc(S["consts2"], 16)

            def load_h(i, b):
                for q in range(2):
                    sp.dma_start(hp[:, b, q], hist_d[reg(i, 16 * q, 1)].rearrange("o d c b w -> (o d c) (b w)")) \
                        .then_inc(S[f"hp_loaded{b}"], 16)

            def load_x1r(i, b):
                for q in range(2):
                    sp.dma_start(x1r[HALF * q:HALF * q + C, b],
                                 x1_d[reg(i, 16 * q, 1)].rearrange("o c b w -> (o c) (b w)")) \
                        .then_inc(S[f"x1r{b}"], 16)

            load_h(0, 0)
            load_h(1, 1)
            load_x1r(0, 0)
            load_x1r(1, 1)
            with sp.Fori(0, 7) as j:
                for b in range(2):
                    sp.wait_ge(S["y_mm"], j * 2 + b + 1)
                    load_h(j * 2 + b + 2, b)
            def store_out(i, b):
                sp.wait_ge(S["summed"], i + 1)
                for q in range(2):
                    sp.dma_start(out[reg(i, 16 * q, 1)].rearrange("o c b w -> (o c) (b w)"),
                                 fin[HALF * q:HALF * q + C, b]).then_inc(S[f"out{b}"], 16)
            with sp.Fori(0, 7) as j:
                for b in range(2):
                    store_out(j * 2 + b, b)
                    load_x1r(j * 2 + b + 2, b)
            for b in range(2):
                store_out(14 + b, b)
            for b in range(2):
                sp.wait_ge(S[f"out{b}"], 32 * 8)

        @block.tensor
        def _(pe):
            pe.wait_ge(S["consts0"], 48)

            def norms(c, b):
                pe.wait_ge(S["y_sq_ready"], c + 1)
                pe.matmul(p_nrm[0:2 * CHUNKS, :], sel_sb[:, c], y0_sq[:, b],
                          start=(c == 0), stop=(c == CHUNKS - 1)).then_inc(S["nrm_done"], 1)

            for c in range(CHUNKS):
                b = c % 2
                pe.wait_ge(S[f"x_in{b}"], 16 * (c // 2 + 1))
                if c >= 2:
                    pe.wait_ge(S["y_sq_ready"], c - 1)
                pe.matmul(p_fc1[b][:, :], w1_sb[:, :], x_in[:, b], start=True, stop=True) \
                    .then_inc(S["fc1_done"], 1)
                if c >= 1:
                    norms(c - 1, 1 - b)
            norms(CHUNKS - 1, 1)

            pe.wait_ge(S["edge_w"], 2)
            pe.wait_ge(S["nrm_ready"], 1)

            def keys(g, b):
                pe.wait_ge(S["xn_ready"], g + 1)
                if later(g):
                    pe.wait_ge(S["topk_done"], g)
                for w in range(WIN):
                    lo, at = NODES * w, NODES * (w // 2)
                    mm = pe.matmul(p_keys[HALF * (w % 2):HALF * (w % 2) + HALF, at:at + NODES],
                                   xl[0:HALF + 1, b, lo:lo + NODES], xr[0:HALF + 1, b, lo:lo + NODES],
                                   start=True, stop=True)
                mm.then_inc(S["keys_done"], 1)

            def edges(g, b, n):
                pe.wait_ge(S[f"y_loaded{b}"], n * 32 + 32)
                for k in range(2):
                    if later(g):
                        pe.wait_ge(S["ab_copied"], g * 2 + (k - 1))
                    for q in range(2):
                        at = 2 * NODES * (2 * k + q)
                        lhs = y_hl[:, b, at:at + 2 * NODES]
                        o = p_ab[k][:, 2 * O * q:2 * O * q + 2 * O]
                        pe.matmul(o, lhs, we_hi[:].rearrange("p a o -> p (a o)"), start=True, stop=False)
                        mm = pe.matmul(o, lhs, we_lo[:].rearrange("p a o -> p (a o)"), start=False, stop=True)
                    mm.then_inc(S["ab_mm"], 1)

            def gather(g, q, b):
                pe.wait_ge(S["onehots"], g * 4 + (q + 1))
                for s in range(2):
                    w = 2 * q + s
                    if q > 0 or later(g):
                        pe.wait_ge(S["gelus"], g * 8 + (w - 1))
                    for h in range(2):
                        o = pz[0:O, 2 * s + h, 0:E9 // 2]
                        rhs = onehot[:, q % 2, s, h * (E9 // 2):(h + 1) * (E9 // 2)]
                        pe.matmul(o, ab_hi[:, b, w], rhs, start=True, stop=False)
                        mm = pe.matmul(o, ab_lo[:, b, w], rhs, start=False, stop=True)
                    mm.then_inc(S["z_done"], 1)

            def fc2(g, b):
                pe.wait_ge(S["maxed"], g * 4 + 4)
                if later(g):
                    pe.wait_ge(S["z2_ready"], g)
                pe.matmul(p_fc2[HALF:TOP, :], w2_sb[:, :], hmax[:, b], start=True, stop=True) \
                    .then_inc(S["fc2_done"], 1)

            def turn(g, b, j, last=False):
                if not (last and b):
                    keys(g + 1, 1 - b)
                    edges(g + 1, 1 - b, j + b)
                pe.wait_ge(S["ab_split"], g + 1)
                for q in range(4):
                    gather(g, q, b)
                fc2(g, b)

            keys(0, 0)
            edges(0, 0, 0)
            turn(0, 0, 0)
            turn(1, 1, 0)
            with pe.Fori(1, GROUPS // 2 - 1) as j:
                for b in range(2):
                    turn(j * 2 + b, b, j)
            for b in range(2):
                turn(GROUPS - 2 + b, b, GROUPS // 2 - 1, last=True)

            pe.wait_ge(S["x1_ready"], GROUPS)
            pe.wait_ge(S["wl_split"], 2)
            pe.wait_ge(S["scan_init"], 6)

            def step(s, x):
                if later(s):
                    pe.wait_ge(S["h_hi"], s * 4 + (2 * x - 2))
                for m in range(2):
                    if later(s):
                        pe.wait_ge(S["tanhs"], s * 16 + (8 * x + 4 * m - 12))
                    for d in range(2):
                        row = s if d == 0 else s * -1 + (H - 1)
                        o = pz[0:TOP, 2 * x + m, NX * d:NX * d + NX]
                        n = 0
                        for src, wgt in ((xh_hi, wl_hi), (xh_hi, wl_lo), (xh_lo, wl_hi)):
                            if n == 6 and m == 0 and d == 0 and later(s):
                                pe.wait_ge(S["h_lo"], s * 4 + (2 * x - 2))
                            for t in range(TAPS):
                                at = (W + 1) * BX * x + t
                                rhs = src[0:TOP, reg(row, 0, 1), at:at + (W + 1) * BX] \
                                    .rearrange("p o (b w) -> p (o b) w", w=W + 1)[:, :, 0:W]
                                mm = pe.matmul(o, wgt[0:TOP, d, m, t], rhs, start=(n == 0), stop=(n == 8))
                                n += 1
                    mm.then_inc(S["gates"], 1)

            for x in range(2):
                step(0, x)
            with pe.Fori(1, H) as s:
                for x in range(2):
                    step(s, x)

            pe.wait_ge(S["wp_ready"], 1)
            pe.wait_ge(S["tanhs"], 16 * H)

            def project(i, b, n):
                pe.wait_ge(S[f"hp_loaded{b}"], n * 32 + 32)
                if later(n):
                    pe.wait_ge(S["y_kept"], i - 1)
                for q in range(2):
                    mm = pe.matmul(ps[b][HALF * q:HALF * q + HALF, :], wp_sb[:, :], hp[:, b, q],
                                   start=True, stop=True)
                mm.then_inc(S["y_mm"], 1)

            project(0, 0, 0)
            project(1, 1, 0)
            with pe.Fori(1, H // 4) as j:
                for b in range(2):
                    project(j * 2 + b, b, j)
            pe.wait_ge(S["fold"], 1)
            for q in range(2):
                mm = pe.matmul(p_comb[:, 4 * q:4 * q + 2], comb_sb[:, q], mv[:, :], start=True, stop=True)
            mm.then_inc(S["comb_mm"], 1)

        @block.scalar
        def _(act):
            act.wait_ge(S["t1_ready"], 2)
            for c in range(CHUNKS):
                b = c % 2
                act.wait_ge(S["fc1_done"], c + 1)
                if c >= 2:
                    act.wait_ge(S[f"y_stored{b}"], 96 * (c // 2))
                    act.wait_ge(S["nrm_done"], c - 1)
                    act.wait_ge(S["y_split"], c - 1)
                act.activation(y0[:, b], p_fc1[b][:, :], ACT.Identity, bias=t1[:, 1:2], scale=col1_sb[:, 1:2]) \
                    .then_inc(S["y_ready"], 1)
                act.activation(y0_sq[:, b], p_fc1[b][:, :], ACT.Square, bias=t1[:, 1:2], scale=col1_sb[:, 1:2]) \
                    .then_inc(S["y_sq_ready"], 1)
            act.wait_ge(S["nrm_done"], CHUNKS)
            act.activation(nrm[:], p_nrm[0:2 * CHUNKS, :], ACT.Sqrt).then_inc(S["nrm_ready"], 1)

            act.wait_ge(S["edge_w"], 2)
            act.wait_ge(S["nrows_stored"], 48)

            def copy_ab(g, b):
                for k in range(2):
                    act.wait_ge(S["ab_mm"], g * 2 + (k + 1))
                    if k == 0 and later(g):
                        act.wait_ge(S["ab_split"], g)
                    bank = p_ab[k][:, 0:4 * O].rearrange("p (q a o) -> p q a o", q=2, a=2)
                    to_windows = ab[:, 4 * k:4 * k + 4].rearrange("p (q s) o -> p q s o", s=2)
                    for s in range(2):
                        rows = slice(HALF * s, HALF * s + HALF)
                        act.activation(to_windows[0:HALF, :, s], bank[rows, :, 1], ACT.Copy)
                        ins = act.activation(to_windows[HALF:P, :, s], bank[rows, :, 0], ACT.Copy)
                    ins.then_inc(S["ab_copied"], 1)

            def gelu(g, q):
                for s in range(2):
                    act.wait_ge(S["z_done"], g * 8 + (2 * q + s + 1))
                    if q >= 2 or later(g):
                        act.wait_ge(S["maxed"], g * 4 + (q - 1))
                    act.activation(gel[:, q % 2, s].rearrange("p (h n) -> p h n", h=2),
                                   pz[0:O, 2 * s:2 * s + 2, 0:E9 // 2], ACT.Gelu).then_inc(S["gelus"], 1)

            def fc2_out(g):
                act.wait_ge(S["fc2_done"], g + 1)
                if later(g):
                    act.wait_ge(S["x1_ready"], g)
                act.activation(z2[HALF:TOP], p_fc2[HALF:TOP, :], ACT.Identity, bias=t2[HALF:TOP, 1:2],
                               scale=col2_sb[HALF:TOP, 1:2]).then_inc(S["z2_ready"], 1)

            def turn(g, b, last=False):
                gelu(g, 0)
                if not (last and b):
                    copy_ab(g + 1, 1 - b)
                for q in range(1, 4):
                    gelu(g, q)
                fc2_out(g)

            copy_ab(0, 0)
            turn(0, 0)
            turn(1, 1)
            with act.Fori(1, GROUPS // 2 - 1) as j:
                for b in range(2):
                    turn(j * 2 + b, b)
            for b in range(2):
                turn(GROUPS - 2 + b, b, last=True)

            act.wait_ge(S["scan_init"], 6)

            def step(s, x, last=False):
                for m, (low, high) in enumerate(((ti, tf), (tg, to))):
                    for d in range(2):
                        if d == 0:
                            act.wait_ge(S["gates"], s * 4 + (2 * x + m + 1))
                        if d == 0 and later(s):
                            if m == 0:
                                act.wait_ge(S["cell_parts"], s * 2 + (x - 1))
                            else:
                                act.wait_ge(S["h2_ready"], s * 4 + (2 * x - 2))
                        for dst, at in ((low, 0), (high, HALF)):
                            act.activation(dst[HALF * d:HALF * d + C, x],
                                           pz[at:at + C, 2 * x + m, NX * d:NX * d + NX], ACT.Tanh) \
                                .then_inc(S["tanhs"], 1)
                act.wait_ge(S["cells"], s * 2 + (x + 1))
                act.activation(tc[0:TOP, x], c2[0:TOP, x], ACT.Tanh, scale=0.5).then_inc(S["tanh_c"], 1)
                if last:
                    return
                for d, row in ((0, s + 1), (1, s * -1 + (H - 2))):
                    act.wait_ge(S["h2_ready"], s * 4 + (2 * x + d + 1))
                    act.activation(h_rows(xh_hi, row, x), h2[:, x, d].rearrange("p (b w) -> p b w", w=W),
                                   ACT.Copy).then_inc(S["h_hi"], 1)

            for x in range(2):
                step(0, x)
            with act.Fori(1, H - 1) as s:
                for x in range(2):
                    step(s, x)
            for x in range(2):
                step(H - 1, x, last=True)

            for x in range(2):
                act.wait_ge(S[f"hist{x}"], 32 * H)

            def keep(i, b):
                act.wait_ge(S["y_mm"], i + 1)
                act.activation(one_row(y_sb, i), ps[b][:, :], ACT.Copy).then_inc(S["y_kept"], 1)

            with act.Fori(0, H // 4) as j:
                for b in range(2):
                    keep(j * 2 + b, b)
            act.wait_ge(S["stat"], 3)
            act.activation(st[:, 3:4], st[:, 2:3], ACT.Sqrt).then_inc(S["stat"], 1)
            act.wait_ge(S["stat"], 8)

            def relu(i, b):
                act.activation(act_y[:, b], one_row(y_sb, i), ACT.Relu, bias=st[:, 7:8], scale=st[:, 5:6]) \
                    .then_inc(S["relus"], 1)

            relu(0, 0)
            relu(1, 1)
            with act.Fori(1, H // 4) as j:
                for b in range(2):
                    act.wait_ge(S["summed"], j * 2 + b - 1)
                    relu(j * 2 + b, b)

        @block.gpsimd
        def _(pool):
            for t in (xh_hi, xh_lo):
                pool.memset(t[:].bitcast(F32), 0.0).then_inc(S["zeros_set"], 1)
            pool.wait_ge(S["zeros_set"], 2)
            pool.memset(xh_hi[32:HALF].bitcast(F32), 1.0).then_inc(S["zeros_set"], 1)
            pool.wait_ge(S["zeros_set"], 3)
            pool.memset(xh_hi[32:C].bitcast(F32), 0.0).then_inc(S["zeros_set"], 1)
            pool.wait_ge(S["nrows_stored"], 48)
            for b in range(2):
                pool.wait_ge(S[f"y_stored{b}"], 96 * CHUNKS // 2)
            pool.memset(y_hl[32:HALF].bitcast(F32), 0.0).then_inc(S["own_set"], 1)
            pool.memset(y_hl[96:P].bitcast(F32), 1.0).then_inc(S["own_set"], 1)
            pool.memset(xl[32:HALF], 0.0).then_inc(S["own_set"], 1)
            pool.memset(xr[32:HALF], 0.0).then_inc(S["own_set"], 1)
            pool.wait_ge(S["own_set"], 4)

            def unit(g, b, n):
                pool.wait_ge(S[f"x_loaded{b}"], n * 64 + 64)
                pool.tensor_tensor(xr[0:C, b], xl[0:C, b], side[0:C, b], ALU.mult).then_inc(S["xn_ready"], 1)

            def split_ab(g, b):
                pool.wait_ge(S["ab_copied"], g * 2 + 2)
                if later(g, 2):
                    pool.wait_ge(S["z_done"], g * 8 - 8)
                    pool.wait_ge(S["x1_ready"], g - 1)
                passed(pool, "pool_passed")
                pool.tensor_scalar(ab_hi[:, b], ab[:], 1.0, 0.0, ALU.mult, ALU.add) \
                    .then_inc(S["ab_hi_ready"], 1)
                pool.wait_ge(S["ab_hi_ready"], g + 1)
                pool.tensor_tensor(ab_lo[:, b], ab[:], ab_hi[:, b].bitcast(F32), ALU.subtract) \
                    .then_inc(S["ab_split"], 1)

            def residual(g, b, n, split_next):
                if split_next:
                    pool.wait_ge(S["ab_split"], g + 2)
                pool.wait_ge(S["z2_ready"], g + 1)
                pool.wait_ge(S[f"xres_loaded{b}"], n * 16 + 16)
                if later(n):
                    pool.wait_ge(S[f"x1_stored{b}"], n * 32)
                pool.tensor_tensor(x1[HALF:TOP, b], z2[HALF:TOP], side[HALF:TOP, b], ALU.add) \
                    .then_inc(S["x1_sum"], 1)
                wr = g // PAIRS
                p = g % PAIRS

                def rows(t, h):
                    return t[HALF:TOP, reg(wr * WS, 0, WS), reg(p * (W + 1), h * PAIRS * (W + 1) + 1, W)]

                def part(t, h):
                    return t.rearrange("c (h r w) -> c h r w", h=2, w=W)[:, h]

                for h in range(2):
                    ins = pool.tensor_tensor(rows(xh_hi, h), part(z2[HALF:TOP], h),
                                             part(side[HALF:TOP, b], h), ALU.add)
                ins.then_inc(S["x1_hi"], 1)
                pool.wait_ge(S["x1_sum"], g + 1)
                pool.wait_ge(S["x1_hi"], g + 1)
                for h in range(2):
                    ins = pool.tensor_tensor(rows(xh_lo, h), part(x1[HALF:TOP, b], h),
                                             rows(xh_hi, h).bitcast(F32), ALU.subtract)
                ins.then_inc(S["x1_ready"], 1)

            def turn(g, b, j, last=False):
                if not (last and b):
                    unit(g + 1, 1 - b, j + b)
                    split_ab(g + 1, 1 - b)
                residual(g, b, j, not (last and b))

            pool.wait_ge(S["zeros_set"], 4)
            unit(0, 0, 0)
            split_ab(0, 0)
            turn(0, 0, 0)
            turn(1, 1, 0)
            with pool.Fori(1, GROUPS // 2 - 1) as j:
                for b in range(2):
                    turn(j * 2 + b, b, j)
            for b in range(2):
                turn(GROUPS - 2 + b, b, GROUPS // 2 - 1, last=True)

        @block.vector
        def _(dve):
            dve.wait_ge(S["consts0"], 48)
            dve.tensor_tensor(t1[:, 0:1], col1_sb[:, 0:1], col1_sb[:, 1:2], ALU.mult).then_inc(S["t1_ready"], 1)
            dve.wait_ge(S["t1_ready"], 1)
            dve.tensor_tensor(t1[:, 1:2], t1[:, 0:1], col1_sb[:, 2:3], ALU.add).then_inc(S["t1_ready"], 1)
            for c in range(CHUNKS):
                b = c % 2
                dve.wait_ge(S["y_ready"], c + 1)
                if c >= 2:
                    dve.wait_ge(S[f"y_stored{b}"], 96 * (c // 2))
                dve.tensor_copy(y0_hi[:, b], y0[:, b]).then_inc(S["y_hi_ready"], 1)
                dve.wait_ge(S["y_hi_ready"], c + 1)
                dve.tensor_tensor(y0_lo[:, b], y0[:, b], y0_hi[:, b].bitcast(F32), ALU.subtract) \
                    .then_inc(S["y_split"], 1)
            dve.wait_ge(S["nrm_ready"], 1)
            dve.tensor_scalar(nmax[:], nrm[:], 1e-12, None, ALU.max).then_inc(S["norm_parts"], 1)
            dve.tensor_scalar(nunit[:], nrm[:], 1e12, 1.0, ALU.mult, ALU.min).then_inc(S["norm_parts"], 1)
            dve.wait_ge(S["norm_parts"], 2)
            dve.reciprocal(nrows[:, 0], nmax[:]).then_inc(S["nrows_ready"], 1)
            dve.tensor_scalar(nrows[:, 1], nmax[:], -0.5, None, ALU.mult).then_inc(S["nrows_ready"], 1)
            dve.tensor_tensor(nrows[:, 2], nunit[:], nunit[:], ALU.mult).then_inc(S["nrows_ready"], 1)

            dve.wait_ge(S["consts1"], 7 * 16)
            EP = S["edge_parts"]
            dve.tensor_tensor(we[:, 0], we_raw[:, 0], we_raw[:, 1], ALU.subtract).then_inc(EP, 1)
            dve.tensor_tensor(we[:, 1], we_raw[:, 1], we_mul[:], ALU.mult).then_inc(EP, 1)
            dve.tensor_tensor(t2[HALF:TOP, 0:1], col2_sb[HALF:TOP, 0:1], col2_sb[HALF:TOP, 1:2], ALU.mult) \
                .then_inc(EP, 1)
            dve.wait_ge(EP, 3)
            dve.tensor_tensor(we[:, 0], we[:, 0], we_mul[:], ALU.mult).then_inc(EP, 1)
            dve.tensor_tensor(t2[HALF:TOP, 1:2], t2[HALF:TOP, 0:1], col2_sb[HALF:TOP, 2:3], ALU.add) \
                .then_inc(EP, 1)
            dve.wait_ge(EP, 5)
            dve.tensor_tensor(we[:], we[:], we_add[:], ALU.add).then_inc(EP, 1)
            dve.wait_ge(EP, 6)
            for k in range(4):
                dve.tensor_copy(onehot[HALF:P, k // 2, k % 2], ab[HALF:P].rearrange("p w n -> p (w n)")[:, 0:E9])
            dve.tensor_copy(we_hi[:], we[:]).then_inc(S["edge_w"], 1)
            dve.wait_ge(S["edge_w"], 1)
            dve.tensor_tensor(we_lo[:], we[:], we_hi[:].bitcast(F32), ALU.subtract).then_inc(S["edge_w"], 1)

            def topk(g, b, n, u):
                if u == 0:
                    dve.wait_ge(S["keys_done"], g + 1)
                    if later(n):
                        dve.wait_ge(S[f"idx_stored{b}"], n * 16)
                    passed(dve, "dve_passed")
                TP = S["topk_parts"]
                k = [p_keys[:, NODES * (2 * u + t):NODES * (2 * u + t) + NODES] for t in range(2)]
                i = [idx[:, b, 2 * u + t] for t in range(2)]
                for t in range(2):
                    ins = dve.max(val8[:, t, 0:8], k[t])
                ins.then_inc(TP, 1)
                dve.wait_ge(TP, g * 6 + (3 * u + 1))
                passed(dve, "dve_passed")
                for t in range(2):
                    dve.max_index(i[t][:, 0:8], val8[:, t, 0:8], k[t])
                for t in range(2):
                    ins = dve.match_replace(keys2[:, t], val8[:, t, 0:8], k[t], LOWEST)
                ins.then_inc(TP, 1)
                dve.wait_ge(TP, g * 6 + (3 * u + 2))
                passed(dve, "dve_passed")
                for t in range(2):
                    ins = dve.max(val8[:, t, 8:16], keys2[:, t])
                ins.then_inc(TP, 1)
                dve.wait_ge(TP, g * 6 + (3 * u + 3))
                passed(dve, "dve_passed")
                for t in range(2):
                    ins = dve.max_index(i[t][:, 8:16], val8[:, t, 8:16], keys2[:, t])
                if u == 1:
                    ins.then_inc(S["topk_done"], 1)

            def one_hot(g, b, n, q):
                if q == 0:
                    dve.wait_ge(S[f"idx_here{b}"], n * 16 + 16)
                if q >= 2 or later(g):
                    dve.wait_ge(S["z_done"], g * 8 + (2 * q - 2))
                at = HALF * b
                dve.tensor_scalar(onehot[0:HALF, q % 2], ib[at:at + HALF, 2 * q:2 * q + 2],
                                  jcol_sb[at:at + HALF, 0:1], None, ALU.is_equal).then_inc(S["onehots"], 1)

            def maxima(g, b, q):
                dve.wait_ge(S["gelus"], g * 8 + (2 * q + 2))
                if q == 0 and later(g, 2):
                    dve.wait_ge(S["fc2_done"], g - 1)
                at = HG * (q // 2) + 2 * WS * (q % 2)
                dst = hmax[:, b, HG * (q // 2):HG * (q // 2) + HG] \
                    .rearrange("p (r w c) -> p w r c", r=WS, c=WS)[:, 2 * (q % 2):2 * (q % 2) + 2]
                dve.tensor_reduce(dst, gel[:, q % 2].rearrange("p w (r c k) -> p w r c k", r=WS, k=K),
                                  AX_X, ALU.max).then_inc(S["maxed"], 1)

            def turn(g, b, j, last=False):
                more = not (last and b)
                one_hot(g, b, j, 0)
                one_hot(g, b, j, 1)
                if more:
                    topk(g + 1, 1 - b, j + b, 0)
                maxima(g, b, 0)
                one_hot(g, b, j, 2)
                if more:
                    topk(g + 1, 1 - b, j + b, 1)
                maxima(g, b, 1)
                one_hot(g, b, j, 3)
                maxima(g, b, 2)
                maxima(g, b, 3)

            topk(0, 0, 0, 0)
            topk(0, 0, 0, 1)
            turn(0, 0, 0)
            turn(1, 1, 0)
            with dve.Fori(1, GROUPS // 2 - 1) as j:
                for b in range(2):
                    turn(j * 2 + b, b, j)
            for b in range(2):
                turn(GROUPS - 2 + b, b, GROUPS // 2 - 1, last=True)

            for b in range(2):
                dve.wait_ge(S[f"x1_stored{b}"], 32 * (GROUPS // 2))
            dve.wait_ge(S["x1_ready"], GROUPS)
            dve.wait_ge(S["zeros_set"], 4)
            for t in (ti, tf, tg, to, c2, tc):
                dve.memset(t[:], 0.0).then_inc(S["scan_init"], 1)
            dve.wait_ge(S["wl_loaded"], 16)
            n = 0
            for aps in ([wl_raw[:, d, 0] for d in range(2)],
                        [wl_raw[:, d, 1, :, HALF:TOP] for d in range(2)],
                        [wl_raw[0:C, d] for d in range(2)]):
                for part in aps:
                    dve.tensor_scalar(part, part, 0.5, None, ALU.mult).then_inc(S["wl_scaled"], 1)
                    n += 1
                dve.wait_ge(S["wl_scaled"], n)
            dve.tensor_copy(wl_hi[:], wl_raw[:]).then_inc(S["wl_split"], 1)
            dve.wait_ge(S["wl_split"], 1)
            dve.tensor_tensor(wl_lo[:], wl_raw[:], wl_hi[:].bitcast(F32), ALU.subtract) \
                .then_inc(S["wl_split"], 1)
            dve.wait_ge(S["scan_init"], 6)

            def step(s, x, last=False):
                dve.wait_ge(S["tanhs"], s * 16 + (8 * x + 4))
                if later(s):
                    dve.wait_ge(S["cells"], s * 2 + (x - 1))
                dve.scalar_tensor_tensor(cu[0:TOP, x], tf[0:TOP, x], 1.0, c2[0:TOP, x], ALU.add, ALU.mult)
                dve.wait_ge(S["tanhs"], s * 16 + (8 * x + 7))
                dve.scalar_tensor_tensor(cv[0:TOP, x], ti[0:TOP, x], 1.0, tg[0:TOP, x], ALU.add, ALU.mult) \
                    .then_inc(S["cell_parts"], 1)
                dve.wait_ge(S["cell_parts"], s * 2 + (x + 1))
                dve.scalar_tensor_tensor(c2[0:TOP, x], cu[0:TOP, x], 0.5, cv[0:TOP, x], ALU.mult, ALU.add) \
                    .then_inc(S["cells"], 1)
                dve.wait_ge(S["tanh_c"], s * 2 + (x + 1))
                if later(s):
                    dve.wait_ge(S[f"hist{x}"], s * 32)
                for d in range(2):
                    at = HALF * d
                    dve.scalar_tensor_tensor(h2[:, x, d], to[at:at + C, x], 1.0, tc[at:at + C, x],
                                             ALU.add, ALU.mult).then_inc(S["h2_ready"], 1)
                if last:
                    return
                for d, row in ((0, s + 1), (1, s * -1 + (H - 2))):
                    dve.wait_ge(S["h_hi"], s * 4 + (2 * x + d + 1))
                    dve.tensor_tensor(h_rows(xh_lo, row, x), h2[:, x, d].rearrange("p (b w) -> p b w", w=W),
                                      h_rows(xh_hi, row, x).bitcast(F32), ALU.subtract).then_inc(S["h_lo"], 1)

            for x in range(2):
                step(0, x)
            with dve.Fori(1, H - 1) as s:
                for x in range(2):
                    step(s, x)
            for x in range(2):
                step(H - 1, x, last=True)

            dve.wait_ge(S["consts2"], 48)
            dve.tensor_scalar(wp_sb[:], wp_sb[:], 0.5, None, ALU.mult).then_inc(S["wp_ready"], 1)

            def stats(i, b):
                dve.wait_ge(S["y_kept"], i + 1)
                dve.bn_stats(one_row(bst, i), one_row(y_sb, i)).then_inc(S["y_stats"], 1)

            with dve.Fori(0, H // 4) as j:
                for b in range(2):
                    stats(j * 2 + b, b)
            dve.wait_ge(S["y_stats"], H // 2)
            dve.bn_aggr(mv[:, :], bst[:].rearrange("p r n -> p (r n)")).then_inc(S["fold"], 1)
            dve.wait_ge(S["comb_mm"], 1)
            ST = S["stat"]
            dve.tensor_copy(st[:, 0:1], p_comb[:, 4:5]).then_inc(ST, 1)
            dve.wait_ge(ST, 1)
            dve.scalar_tensor_tensor(st[:, 1:2], st[:, 0:1], st[:, 0:1], p_comb[:, 1:2], ALU.mult, ALU.add) \
                .then_inc(ST, 1)
            dve.wait_ge(ST, 2)
            dve.tensor_scalar(st[:, 2:3], st[:, 1:2], EPS, None, ALU.add).then_inc(ST, 1)
            dve.wait_ge(ST, 4)
            dve.reciprocal(st[:, 4:5], st[:, 3:4]).then_inc(ST, 1)
            dve.wait_ge(ST, 5)
            dve.tensor_tensor(st[:, 5:6], st[:, 4:5], gb_sb[:, 0:1], ALU.mult).then_inc(ST, 1)
            dve.wait_ge(ST, 6)
            dve.tensor_tensor(st[:, 6:7], st[:, 5:6], p_comb[:, 0:1], ALU.mult).then_inc(ST, 1)
            dve.wait_ge(ST, 7)
            dve.tensor_tensor(st[:, 7:8], gb_sb[:, 1:2], st[:, 6:7], ALU.subtract).then_inc(ST, 1)

            def add(i, b, n):
                dve.wait_ge(S["relus"], i + 1)
                dve.wait_ge(S[f"x1r{b}"], n * 32 + 32)
                if later(n):
                    dve.wait_ge(S[f"out{b}"], n * 32)
                for h in range(2):
                    at = HALF * h
                    ins = dve.tensor_tensor(fin[at:at + C, b], act_y[at:at + C, b], x1r[at:at + C, b], ALU.add)
                ins.then_inc(S["summed"], 1)

            for b in range(2):
                add(b, b, 0)
            with dve.Fori(1, H // 4) as j:
                for b in range(2):
                    add(j * 2 + b, b, j)


def kernel(**inputs):
    import numpy as np
    import concourse.bacc as bacc
    from concourse.bass_utils import run_bass_kernel_spmd

    f = {k: np.asarray(v) for k, v in inputs.items()}
    z = np.zeros

    def halves(cols):
        t = z((P, cols.shape[1]), np.float32)
        t[0:C] = t[HALF:TOP] = cols
        return t

    x = f["x"].reshape(2, PAIRS, C, WROWS, WS, W // WS, WS)
    xs = z((P, CHUNKS, CHUNK), np.float32)
    by_window = x.transpose(0, 2, 3, 1, 5, 4, 6).reshape(2, C, CHUNKS, CHUNK)
    xs[0:C], xs[HALF:TOP] = by_window[0], by_window[1]
    xrow = x.transpose(2, 3, 1, 0, 4, 5, 6).reshape(C, GROUPS, GN)
    w1 = z((P, P), np.float32)
    w1[0:C, 0:C] = w1[HALF:TOP, HALF:TOP] = f["L0_conv_fc1_w"].T
    ones_sel = z((P, CHUNKS, 2 * CHUNKS), np.float32)
    for c in range(CHUNKS):
        ones_sel[0:C, c, 2 * c] = ones_sel[HALF:TOP, c, 2 * c + 1] = 1.0
    col1 = halves(np.stack([f["L0_conv_fc1_b"], f["L0_conv_fc1_s"], f["L0_conv_fc1_t"]], 1))
    col2 = halves(np.stack([f["L0_conv_fc2_b"], f["L0_conv_fc2_s"], f["L0_conv_fc2_t"]], 1))
    jcol = (np.arange(P, dtype=np.float32) % NODES).reshape(P, 1)
    ewt = f["L0_conv_ew"].T.reshape(2, C, O)
    wedge = z((P, 2, O), np.float32)
    wedge[0:C] = wedge[HALF:TOP] = ewt.transpose(1, 0, 2)
    wedge[TOP, 0] = f["L0_conv_eb"]
    edge_shift = z((P, 2, O), np.float32)
    edge_shift[TOP, 0] = f["L0_conv_et"]
    ident9 = np.repeat(np.eye(NODES, dtype=np.float32), K, axis=1)
    w2 = np.ascontiguousarray(f["L0_conv_fc2_w"].T)
    wl = z((P, 2, 2, TAPS, TOP), np.float32)
    for d, (wn, bn) in enumerate((("L1_conv_w_f", "L1_conv_b_f"), ("L1_conv_w_b", "L1_conv_b_b"))):
        mid = f[wn][:, :, 1, :].reshape(4, C, 2, C, TAPS)
        for gate in range(4):
            m, at = gate // 2, HALF * (gate % 2)
            t = mid[gate].transpose(1, 2, 3, 0)
            wl[HALF:TOP, d, m, :, at:at + C] = t[0]
            wl[0:C, d, m, :, at:at + C] = t[1]
            wl[C, d, m, 1, at:at + C] = f[bn].reshape(4, C)[gate]
    wp = z((O, HALF), np.float32)
    wp[:, 0:C] = f["L1_conv_w_proj"].T
    gb = halves(np.stack([f["L1_conv_gamma"], f["L1_conv_beta"]], 1))
    comb = z((P, 2, P), np.float32)
    for c in range(HALF):
        for q in range(2):
            for r in range(2):
                comb[HALF * q + c, 0, HALF * r + c] = 0.5
                comb[HALF * q + c, 1, HALF * r + c] = 0.5 - q

    arrays = dict(xs=xs, xrow=xrow, w1=w1, ones_sel=ones_sel, col1=col1, jcol=jcol, wedge=wedge,
                  edge_scale=f["L0_conv_es"], edge_shift=edge_shift, ident9=ident9, w2=w2, col2=col2,
                  wl=wl, wp=wp, gb=gb, comb=comb)
    arrays = {k: np.ascontiguousarray(v) for k, v in arrays.items()}
    nc = bacc.Bacc("TRN2", target_bir_lowering=False, num_devices=1)
    aps = {k: nc.dram_tensor(k, v.shape, F32, kind="ExternalInput").ap()
           for k, v in arrays.items()}
    out = nc.dram_tensor("out", (H, C, B, W), F32, kind="ExternalOutput").ap()
    build(nc, **aps, out=out)
    r = run_bass_kernel_spmd(nc, [arrays], core_ids=[0])
    return r.results[0]["out"].transpose(2, 1, 0, 3)
```

```python
from contextlib import ExitStack

import concourse.bass as bass
from concourse import mybir

F32 = mybir.dt.float32
F32R = mybir.dt.float32r
U16 = mybir.dt.uint16
ALU = mybir.AluOpType
ACT = mybir.ActivationFunctionType
AX_X = mybir.AxisListType.X

P = 128
B, C, H, W = 16, 48, 32, 32
O = 2 * C
WS = 8
NODES = WS * WS
K = 9
PAIRS = B // 2
WROWS = H // WS
GROUPS = WROWS * PAIRS
WIN = 2 * (W // WS)
GN = WIN * NODES
HG = GN // 2
CHUNK = 512
CHUNKS = GROUPS * HG // CHUNK
HALF = 64
TOP = HALF + C
E9 = NODES * K
SLOT = (W + 1) * B + 2
TAPS = 3
BX = B // 2
NX = BX * W
EPS = 1e-5
LOWEST = -3.0e38


def split(t):
    return t.rearrange("p (h n) -> p h n", h=2)


def build(nc, xs, xrow, w1, ones_sel, col1, jcol, wedge, edge_scale, edge_shift, ident9, w2, col2,
          wl, wp, gb, comb, out):
    yf_d = nc.dram_tensor("yf_d", [C, GROUPS, 2, HG], F32, kind="Internal").ap()
    yhi_d = nc.dram_tensor("yhi_d", [C, GROUPS, 2, HG], F32, kind="Internal").ap()
    ylo_d = nc.dram_tensor("ylo_d", [C, GROUPS, 2, HG], F32, kind="Internal").ap()
    nr_d = nc.dram_tensor("nr_d", [3, CHUNKS, 2, 2, HG], F32, kind="Internal").ap()
    idx_d = nc.dram_tensor("idx_d", [GROUPS, WIN, NODES, K], U16, kind="Internal").ap()
    x1_d = nc.dram_tensor("x1_d", [H, C, B, W], F32, kind="Internal").ap()
    hist_d = nc.dram_tensor("hist_d", [H, 2, C, B, W], F32, kind="Internal").ap()

    with ExitStack() as ctx:
        def sem(name):
            return ctx.enter_context(nc.semaphore(name))

        def sb_in(stack):
            return lambda name, shape, dt: stack.enter_context(nc.sbuf_tensor(name, shape, dt))

        sb = sb_in(ctx)
        xh_hi = sb("xh_hi", [P, H, SLOT], F32R)
        xh_lo = sb("xh_lo", [P, H, SLOT], F32R)

        with ExitStack() as s0:
            a = sb_in(s0)
            x_in = a("x_in", [P, 2, CHUNK], F32)
            w1_sb = a("w1_sb", [P, P], F32)
            sel_sb = a("sel_sb", [P, CHUNKS, 2 * CHUNKS], F32)
            col1_sb = a("col1_sb", [P, 3], F32)
            t1 = a("t1", [P, 2], F32)
            y0 = a("y0", [P, 2, CHUNK], F32)
            y0_hi = a("y0_hi", [P, 2, CHUNK], F32R)
            y0_lo = a("y0_lo", [P, 2, CHUNK], F32R)
            y0_sq = a("y0_sq", [P, 2, CHUNK], F32)
            nrm = a("nrm", [2 * CHUNKS, CHUNK], F32)
            nmax = a("nmax", [2 * CHUNKS, CHUNK], F32)
            nunit = a("nunit", [2 * CHUNKS, CHUNK], F32)
            nrows = a("nrows", [2 * CHUNKS, 3, CHUNK], F32)

        with ExitStack() as s1:
            a = sb_in(s1)
            y_hl = a("y_hl", [P, 2, GN], F32R)
            xl = a("xl", [P, 2, GN], F32)
            xr = a("xr", [P, 2, GN], F32)
            side = a("side", [P, 2, GN], F32)
            ib = a("ib", [P, WIN, E9], U16)
            keys2 = a("keys2", [P, 4, NODES], F32)
            val8 = a("val8", [P, 4, 16], F32)
            idx = a("idx", [P, 2, 4, 16], U16)
            onehot = a("onehot", [P, 2, 2, E9], F32R)
            gel = a("gel", [O, 2, 2, E9], F32)
            hmax = a("hmax", [O, 2, GN], F32)
            ab = a("ab", [P, WIN, O], F32)
            ab_hi = a("ab_hi", [P, 2, WIN, O], F32R)
            ab_lo = a("ab_lo", [P, 2, WIN, O], F32R)
            jcol_sb = a("jcol_sb", [P, 1], F32)
            we_raw = a("we_raw", [P, 2, O], F32)
            we_mul = a("we_mul", [P, O], F32)
            we_add = a("we_add", [P, 2, O], F32)
            we = a("we", [P, 2, O], F32)
            we_hi = a("we_hi", [P, 2, O], F32R)
            we_lo = a("we_lo", [P, 2, O], F32R)
            w2_sb = a("w2_sb", [O, C], F32)
            col2_sb = a("col2_sb", [P, 3], F32)
            t2 = a("t2", [P, 2], F32)
            z2 = a("z2", [P, GN], F32)
            x1 = a("x1", [P, 2, GN], F32)

        with ExitStack() as s2:
            a = sb_in(s2)
            wl_raw = a("wl_raw", [P, 2, 2, TAPS, TOP], F32)
            wl_hi = a("wl_hi", [P, 2, 2, TAPS, TOP], F32R)
            wl_lo = a("wl_lo", [P, 2, 2, TAPS, TOP], F32R)
            ti = a("ti", [P, 2, NX], F32)
            tf = a("tf", [P, 2, NX], F32)
            tg = a("tg", [P, 2, NX], F32)
            to = a("to", [P, 2, NX], F32)
            cu = a("cu", [P, 2, NX], F32)
            cv = a("cv", [P, 2, NX], F32)
            c2 = a("c2", [P, 2, NX], F32)
            tc = a("tc", [P, 2, NX], F32)
            h2 = a("h2", [C, 2, 2, NX], F32)

        with ExitStack() as s3:
            a = sb_in(s3)
            wp_sb = a("wp_sb", [O, HALF], F32)
            gb_sb = a("gb_sb", [P, 2], F32)
            comb_sb = a("comb_sb", [P, 2, P], F32)
            hp = a("hp", [O, 2, 2, B * W], F32)
            y_sb = a("y_sb", [P, H // 2, B * W], F32)
            bst = a("bst", [P, H // 2, 6], F32)
            mv = a("mv", [P, 2], F32)
            st = a("st", [P, 8], F32)
            x1r = a("x1r", [P, 2, B * W], F32)
            act_y = a("act_y", [P, 2, B * W], F32)
            fin = a("fin", [P, 2, B * W], F32)

        pz = ctx.enter_context(nc.psum_tensor("pz", [P, 4, 512], F32))
        ps = [ctx.enter_context(nc.psum_tensor(f"ps{i}", [P, 512], F32)) for i in range(4)]
        p_fc1 = ps[0:2]
        p_nrm = ps[2]
        p_keys = ps[0]
        p_ab = ps[1:3]
        p_fc2 = ps[3]
        p_comb = ps[2]

        names = """pool_passed dve_passed consts0 x_in0 x_in1 fc1_done y_ready y_sq_ready nrm_done y_hi_ready y_split
            y_stored0 y_stored1 nrm_ready norm_parts nrows_ready nrows_stored t1_ready zeros_set
            consts1 edge_parts edge_w y_loaded0 y_loaded1 x_loaded0 x_loaded1 xres_loaded0 xres_loaded1
            ab_mm ab_copied ab_hi_ready ab_split xn_ready keys_done topk_done topk_parts idx_stored0
            idx_stored1 idx_here0 idx_here1 onehots z_done gelus maxed fc2_done z2_ready x1_ready
            x1_stored0 x1_stored1 x1_sum x1_hi own_set
            wl_loaded wl_scaled wl_split scan_init gates tanhs cells cell_parts tanh_c h2_ready h_hi
            h_lo hist0 hist1
            consts2 wp_ready hp_loaded0 hp_loaded1 y_mm y_kept y_stats fold comb_mm stat x1r0 x1r1
            relus summed out0 out1""".split()
        S = {n: sem(n) for n in names}
        block = ctx.enter_context(nc.Block())

        def reg(v, lo, n):
            return slice(v + lo, v + lo + n) if isinstance(v, int) else bass.ds(v + lo, n)

        def later(v, n=1):
            return not isinstance(v, int) or v >= n

        def nth(j, b, k):
            return j * 2 + (b + k), (b + k) % 2, j + (b + k) // 2

        def exists(g):
            return not isinstance(g, int) or 0 <= g < GROUPS

        def turns(engine, turn):
            for b in range(2):
                turn(0, b)
            with engine.Fori(1, GROUPS // 2 - 2) as j:
                for b in range(2):
                    turn(j, b)
            for j in (GROUPS // 2 - 2, GROUPS // 2 - 1):
                for b in range(2):
                    turn(j, b)

        def passed(engine, name):
            engine.sem_inc(S[name], 1)

        def one_row(t, i):
            return t[:, reg(i, 0, 1)].rearrange("p o n -> p (o n)")

        def h_rows(t, row, x):
            at = (W + 1) * BX * x + 1
            return t[0:C, reg(row, 0, 1), at:at + (W + 1) * BX] \
                .rearrange("p o (b w) -> p (o b) w", w=W + 1)[:, :, 0:W]

        @block.sync
        def _(sp):
            sp.dma_start(w1_sb[:], w1).then_inc(S["consts0"], 16)
            sp.dma_start(sel_sb[:], ones_sel).then_inc(S["consts0"], 16)
            sp.dma_start(col1_sb[:], col1).then_inc(S["consts0"], 16)

            def load_x(c, b):
                sp.dma_start(x_in[:, b], xs[:, reg(c, 0, 1)].rearrange("p o n -> p (o n)")) \
                    .then_inc(S[f"x_in{b}"], 16)

            def store_y(c, b, src, dst):
                for h in range(2):
                    sp.dma_start(dst[:, reg(c * 2, 0, 2), h],
                                 split(src[HALF * h:HALF * h + C, b].bitcast(F32))).then_inc(S[f"y_stored{b}"], 16)

            load_x(0, 0)
            load_x(1, 1)
            with sp.Fori(0, CHUNKS // 2 - 1) as j:
                for b in range(2):
                    sp.wait_ge(S["y_split"], j * 2 + b + 1)
                    store_y(j * 2 + b, b, y0, yf_d)
                    store_y(j * 2 + b, b, y0_hi, yhi_d)
                    store_y(j * 2 + b, b, y0_lo, ylo_d)
                    sp.wait_ge(S["fc1_done"], j * 2 + b + 1)
                    load_x(j * 2 + 2 + b, b)
            for b in range(2):
                c = CHUNKS - 2 + b
                sp.wait_ge(S["y_split"], c + 1)
                store_y(c, b, y0, yf_d)
                store_y(c, b, y0_hi, yhi_d)
                store_y(c, b, y0_lo, ylo_d)
            sp.wait_ge(S["nrows_ready"], 3)
            for q in range(3):
                sp.dma_start(nr_d[q].rearrange("c h g n -> (c h) (g n)"), nrows[:, q]) \
                    .then_inc(S["nrows_stored"], 16)
            sp.wait_ge(S["nrows_stored"], 48)
            for b in range(2):
                sp.wait_ge(S[f"y_stored{b}"], 6 * 16 * CHUNKS // 2)

            sp.dma_start(jcol_sb[:], jcol).then_inc(S["consts1"], 16)
            sp.dma_start(we_raw[:], wedge).then_inc(S["consts1"], 16)
            sp.dma_start(we_mul[:], edge_scale.rearrange("(o n) -> o n", o=1).to_broadcast([P, O])) \
                .then_inc(S["consts1"], 16)
            sp.dma_start(we_add[:], edge_shift).then_inc(S["consts1"], 16)
            sp.dma_start(w2_sb[:], w2).then_inc(S["consts1"], 16)
            sp.dma_start(col2_sb[:], col2).then_inc(S["consts1"], 16)
            sp.dma_start(ab[HALF:P].rearrange("p w n -> p (w n)")[:, 0:E9], ident9).then_inc(S["consts1"], 16)

            sp.wait_ge(S["own_set"], 4)

            def load_y(g, b, n):
                if later(g, 2):
                    sp.wait_ge(S["ab_mm"], g * 2 - 2)
                for src, at in ((yhi_d, 0), (ylo_d, HALF)):
                    sp.dma_start(y_hl[at:at + C, b].bitcast(F32), src[:, reg(g, 0, 1)].rearrange("c o h n -> c (o h n)")) \
                        .then_inc(S[f"y_loaded{b}"], 16)

            def load_x(g, b, n):
                if later(g, 2):
                    sp.wait_ge(S["keys_done"], g - 1)
                sp.dma_start(xl[0:C, b], yf_d[:, reg(g, 0, 1)].rearrange("c o h n -> c (o h n)")) \
                    .then_inc(S[f"x_loaded{b}"], 16)
                for q, dst in ((0, side[0:C, b]), (1, xl[HALF:HALF + 1, b]), (2, xr[HALF:HALF + 1, b])):
                    src = nr_d[q, reg(n, 0, 1), :, b]
                    if q == 0:
                        src = src.to_broadcast([C, 2, HG])
                    sp.dma_start(split(dst), src).then_inc(S[f"x_loaded{b}"], 16)

            def load_xres(g, b, n):
                sp.dma_start(side[HALF:TOP, b], xrow[:, reg(g, 0, 1)].rearrange("c o n -> c (o n)")) \
                    .then_inc(S[f"xres_loaded{b}"], 16)

            def pass_idx(g, b, n):
                sp.wait_ge(S["topk_done"], g + 1)
                sp.dma_start(idx_d[reg(g, 0, 1)].rearrange("o (t s) n k -> (o s n) t k", s=2),
                             idx[:, b, :, 0:K]).then_inc(S[f"idx_stored{b}"], 16)
                sp.wait_ge(S[f"idx_stored{b}"], n * 16 + 16)
                sp.dma_start(ib[HALF * b:HALF * b + HALF],
                             idx_d[reg(g, 0, 1)].rearrange("o w n k -> o w (n k)")
                             .to_broadcast([HALF, WIN, E9])).then_inc(S[f"idx_here{b}"], 16)

            def store_x1(g, b, n):
                sp.wait_ge(S["x1_ready"], g + 1)
                wr = g // PAIRS
                p = g % PAIRS
                for h in range(2):
                    dst = x1_d[reg(wr * WS, 0, WS), :, reg(p, h * PAIRS, 1)]
                    sp.dma_start(dst.rearrange("r c o w -> c (r o) w"),
                                 x1[HALF:TOP, b].rearrange("c (h r w) -> c h r w", h=2, w=W)[:, h]) \
                        .then_inc(S[f"x1_stored{b}"], 16)

            load_x(0, 0, 0)
            load_y(0, 0, 0)
            load_x(1, 1, 0)
            load_y(1, 1, 0)
            load_xres(0, 0, 0)
            pass_idx(0, 0, 0)
            load_x(2, 0, 1)
            pass_idx(1, 1, 0)
            load_x(3, 1, 1)

            def turn(j, b):
                for k, stage in ((2, load_y), (2, pass_idx), (4, load_x), (-1, store_x1), (1, load_xres)):
                    if exists(nth(j, b, k)[0]):
                        stage(*nth(j, b, k))

            turns(sp, turn)
            store_x1(GROUPS - 1, 1, GROUPS // 2 - 1)
            for b in range(2):
                sp.wait_ge(S[f"x1_stored{b}"], 32 * (GROUPS // 2))

            sp.dma_start(wl_raw[:], wl).then_inc(S["wl_loaded"], 16)

            def store_h(s, x):
                sp.wait_ge(S["h2_ready"], s * 4 + (2 * x + 2))
                for d, row in ((0, s), (1, s * -1 + (H - 1))):
                    dst = hist_d[reg(row, 0, 1), d, :, BX * x:BX * x + BX].rearrange("o c b w -> (o c) (b w)")
                    sp.dma_start(dst, h2[:, x, d]).then_inc(S[f"hist{x}"], 16)

            with sp.Fori(0, H) as s:
                for x in range(2):
                    store_h(s, x)
            for x in range(2):
                sp.wait_ge(S[f"hist{x}"], 32 * H)

            sp.dma_start(wp_sb[:], wp).then_inc(S["consts2"], 16)
            sp.dma_start(gb_sb[:], gb).then_inc(S["consts2"], 16)
            sp.dma_start(comb_sb[:], comb).then_inc(S["consts2"], 16)

            def load_h(i, b):
                for q in range(2):
                    sp.dma_start(hp[:, b, q], hist_d[reg(i, 16 * q, 1)].rearrange("o d c b w -> (o d c) (b w)")) \
                        .then_inc(S[f"hp_loaded{b}"], 16)

            def load_x1r(i, b):
                for q in range(2):
                    sp.dma_start(x1r[HALF * q:HALF * q + C, b],
                                 x1_d[reg(i, 16 * q, 1)].rearrange("o c b w -> (o c) (b w)")) \
                        .then_inc(S[f"x1r{b}"], 16)

            load_h(0, 0)
            load_h(1, 1)
            load_x1r(0, 0)
            load_x1r(1, 1)
            with sp.Fori(0, 7) as j:
                for b in range(2):
                    sp.wait_ge(S["y_mm"], j * 2 + b + 1)
                    load_h(j * 2 + b + 2, b)
            def store_out(i, b):
                sp.wait_ge(S["summed"], i + 1)
                for q in range(2):
                    sp.dma_start(out[reg(i, 16 * q, 1)].rearrange("o c b w -> (o c) (b w)"),
                                 fin[HALF * q:HALF * q + C, b]).then_inc(S[f"out{b}"], 16)
            with sp.Fori(0, 7) as j:
                for b in range(2):
                    store_out(j * 2 + b, b)
                    load_x1r(j * 2 + b + 2, b)
            for b in range(2):
                store_out(14 + b, b)
            for b in range(2):
                sp.wait_ge(S[f"out{b}"], 32 * 8)

        @block.tensor
        def _(pe):
            pe.wait_ge(S["consts0"], 48)

            def norms(c, b):
                pe.wait_ge(S["y_sq_ready"], c + 1)
                pe.matmul(p_nrm[0:2 * CHUNKS, :], sel_sb[:, c], y0_sq[:, b],
                          start=(c == 0), stop=(c == CHUNKS - 1)).then_inc(S["nrm_done"], 1)

            for c in range(CHUNKS):
                b = c % 2
                pe.wait_ge(S[f"x_in{b}"], 16 * (c // 2 + 1))
                if c >= 2:
                    pe.wait_ge(S["y_sq_ready"], c - 1)
                pe.matmul(p_fc1[b][:, :], w1_sb[:, :], x_in[:, b], start=True, stop=True) \
                    .then_inc(S["fc1_done"], 1)
                if c >= 1:
                    norms(c - 1, 1 - b)
            norms(CHUNKS - 1, 1)

            pe.wait_ge(S["edge_w"], 2)
            pe.wait_ge(S["nrm_ready"], 1)

            def keys(g, b, n):
                pe.wait_ge(S["xn_ready"], g + 1)
                if later(g):
                    pe.wait_ge(S["topk_parts"], g * 3 - 1)
                for w in range(WIN):
                    lo, at = NODES * w, NODES * (w // 2)
                    mm = pe.matmul(p_keys[HALF * (w % 2):HALF * (w % 2) + HALF, at:at + NODES],
                                   xl[0:HALF + 1, b, lo:lo + NODES], xr[0:HALF + 1, b, lo:lo + NODES],
                                   start=True, stop=True)
                mm.then_inc(S["keys_done"], 1)

            def edges(g, b, n):
                pe.wait_ge(S[f"y_loaded{b}"], n * 32 + 32)
                for k in range(2):
                    if later(g):
                        pe.wait_ge(S["ab_copied"], g * 2 + (k - 1))
                    for q in range(2):
                        at = 2 * NODES * (2 * k + q)
                        lhs = y_hl[:, b, at:at + 2 * NODES]
                        o = p_ab[k][:, 2 * O * q:2 * O * q + 2 * O]
                        pe.matmul(o, lhs, we_hi[:].rearrange("p a o -> p (a o)"), start=True, stop=False)
                        mm = pe.matmul(o, lhs, we_lo[:].rearrange("p a o -> p (a o)"), start=False, stop=True)
                    mm.then_inc(S["ab_mm"], 1)

            def gather(g, q, b):
                if q == 0:
                    pe.wait_ge(S["ab_split"], g + 1)
                pe.wait_ge(S["onehots"], g * 4 + (q + 1))
                for s in range(2):
                    w = 2 * q + s
                    if q > 0 or later(g):
                        pe.wait_ge(S["gelus"], g * 8 + (w - 1))
                    for h in range(2):
                        o = pz[0:O, 2 * s + h, 0:E9 // 2]
                        rhs = onehot[:, q % 2, s, h * (E9 // 2):(h + 1) * (E9 // 2)]
                        pe.matmul(o, ab_hi[:, b, w], rhs, start=True, stop=False)
                        mm = pe.matmul(o, ab_lo[:, b, w], rhs, start=False, stop=True)
                    mm.then_inc(S["z_done"], 1)

            def fc2(g, b, n):
                pe.wait_ge(S["maxed"], g * 4 + 4)
                if later(g):
                    pe.wait_ge(S["z2_ready"], g)
                pe.matmul(p_fc2[HALF:TOP, :], w2_sb[:, :], hmax[:, b], start=True, stop=True) \
                    .then_inc(S["fc2_done"], 1)

            def turn(j, b):
                def gathers(*which):
                    for k, q in which:
                        g, buf, _ = nth(j, b, k)
                        if exists(g):
                            gather(g, q, buf)

                for k, stage in ((1, edges), (-1, fc2)):
                    if exists(nth(j, b, k)[0]):
                        stage(*nth(j, b, k))
                gathers((0, 2), (0, 3))
                if exists(nth(j, b, 3)[0]):
                    keys(*nth(j, b, 3))
                gathers((1, 0), (1, 1))

            keys(0, 0, 0)
            edges(0, 0, 0)
            keys(1, 1, 0)
            keys(2, 0, 1)
            for q in range(2):
                gather(0, q, 0)
            turns(pe, turn)
            fc2(GROUPS - 1, 1, GROUPS // 2 - 1)

            pe.wait_ge(S["x1_ready"], GROUPS)
            pe.wait_ge(S["wl_split"], 2)
            pe.wait_ge(S["scan_init"], 6)

            def step(s, x):
                if later(s):
                    pe.wait_ge(S["h_hi"], s * 4 + (2 * x - 2))
                for m in range(2):
                    if later(s):
                        pe.wait_ge(S["tanhs"], s * 16 + (8 * x + 4 * m - 12))
                    for d in range(2):
                        row = s if d == 0 else s * -1 + (H - 1)
                        o = pz[0:TOP, 2 * x + m, NX * d:NX * d + NX]
                        n = 0
                        for src, wgt in ((xh_hi, wl_hi), (xh_hi, wl_lo), (xh_lo, wl_hi)):
                            if n == 6 and m == 0 and d == 0 and later(s):
                                pe.wait_ge(S["h_lo"], s * 4 + (2 * x - 2))
                            for t in range(TAPS):
                                at = (W + 1) * BX * x + t
                                rhs = src[0:TOP, reg(row, 0, 1), at:at + (W + 1) * BX] \
                                    .rearrange("p o (b w) -> p (o b) w", w=W + 1)[:, :, 0:W]
                                mm = pe.matmul(o, wgt[0:TOP, d, m, t], rhs, start=(n == 0), stop=(n == 8))
                                n += 1
                    mm.then_inc(S["gates"], 1)

            for x in range(2):
                step(0, x)
            with pe.Fori(1, H) as s:
                for x in range(2):
                    step(s, x)

            pe.wait_ge(S["wp_ready"], 1)
            pe.wait_ge(S["tanhs"], 16 * H)

            def project(i, b, n):
                pe.wait_ge(S[f"hp_loaded{b}"], n * 32 + 32)
                if later(n):
                    pe.wait_ge(S["y_kept"], i - 1)
                for q in range(2):
                    mm = pe.matmul(ps[b][HALF * q:HALF * q + HALF, :], wp_sb[:, :], hp[:, b, q],
                                   start=True, stop=True)
                mm.then_inc(S["y_mm"], 1)

            project(0, 0, 0)
            project(1, 1, 0)
            with pe.Fori(1, H // 4) as j:
                for b in range(2):
                    project(j * 2 + b, b, j)
            pe.wait_ge(S["fold"], 1)
            for q in range(2):
                mm = pe.matmul(p_comb[:, 4 * q:4 * q + 2], comb_sb[:, q], mv[:, :], start=True, stop=True)
            mm.then_inc(S["comb_mm"], 1)

        @block.scalar
        def _(act):
            act.wait_ge(S["t1_ready"], 2)
            for c in range(CHUNKS):
                b = c % 2
                act.wait_ge(S["fc1_done"], c + 1)
                if c >= 2:
                    act.wait_ge(S[f"y_stored{b}"], 96 * (c // 2))
                    act.wait_ge(S["nrm_done"], c - 1)
                    act.wait_ge(S["y_split"], c - 1)
                act.activation(y0[:, b], p_fc1[b][:, :], ACT.Identity, bias=t1[:, 1:2], scale=col1_sb[:, 1:2]) \
                    .then_inc(S["y_ready"], 1)
                act.activation(y0_sq[:, b], p_fc1[b][:, :], ACT.Square, bias=t1[:, 1:2], scale=col1_sb[:, 1:2]) \
                    .then_inc(S["y_sq_ready"], 1)
            act.wait_ge(S["nrm_done"], CHUNKS)
            act.activation(nrm[:], p_nrm[0:2 * CHUNKS, :], ACT.Sqrt).then_inc(S["nrm_ready"], 1)

            act.wait_ge(S["edge_w"], 2)
            act.wait_ge(S["nrows_stored"], 48)

            def copy_ab(g):
                for k in range(2):
                    act.wait_ge(S["ab_mm"], g * 2 + (k + 1))
                    if k == 0 and later(g):
                        act.wait_ge(S["ab_split"], g)
                    bank = p_ab[k][:, 0:4 * O].rearrange("p (q a o) -> p q a o", q=2, a=2)
                    to_windows = ab[:, 4 * k:4 * k + 4].rearrange("p (q s) o -> p q s o", s=2)
                    for s in range(2):
                        rows = slice(HALF * s, HALF * s + HALF)
                        act.activation(to_windows[0:HALF, :, s], bank[rows, :, 1], ACT.Copy)
                        ins = act.activation(to_windows[HALF:P, :, s], bank[rows, :, 0], ACT.Copy)
                    ins.then_inc(S["ab_copied"], 1)

            def gelu(g, q):
                for s in range(2):
                    act.wait_ge(S["z_done"], g * 8 + (2 * q + s + 1))
                    if q >= 2 or later(g):
                        act.wait_ge(S["maxed"], g * 4 + (q - 1))
                    act.activation(gel[:, q % 2, s].rearrange("p (h n) -> p h n", h=2),
                                   pz[0:O, 2 * s:2 * s + 2, 0:E9 // 2], ACT.Gelu).then_inc(S["gelus"], 1)

            def fc2_out(g):
                act.wait_ge(S["fc2_done"], g + 1)
                if later(g):
                    act.wait_ge(S["x1_ready"], g)
                act.activation(z2[HALF:TOP], p_fc2[HALF:TOP, :], ACT.Identity, bias=t2[HALF:TOP, 1:2],
                               scale=col2_sb[HALF:TOP, 1:2]).then_inc(S["z2_ready"], 1)

            def turn(j, b):
                if exists(nth(j, b, 1)[0]):
                    copy_ab(nth(j, b, 1)[0])
                if exists(nth(j, b, -1)[0]):
                    fc2_out(nth(j, b, -1)[0])
                for k, q in ((0, 2), (0, 3), (1, 0), (1, 1)):
                    if exists(nth(j, b, k)[0]):
                        gelu(nth(j, b, k)[0], q)

            copy_ab(0)
            for q in range(2):
                gelu(0, q)
            turns(act, turn)
            fc2_out(GROUPS - 1)

            act.wait_ge(S["scan_init"], 6)

            def step(s, x, last=False):
                for m, (low, high) in enumerate(((ti, tf), (tg, to))):
                    for d in range(2):
                        if d == 0:
                            act.wait_ge(S["gates"], s * 4 + (2 * x + m + 1))
                        if d == 0 and later(s):
                            if m == 0:
                                act.wait_ge(S["cell_parts"], s * 2 + (x - 1))
                            else:
                                act.wait_ge(S["h2_ready"], s * 4 + (2 * x - 2))
                        for dst, at in ((low, 0), (high, HALF)):
                            act.activation(dst[HALF * d:HALF * d + C, x],
                                           pz[at:at + C, 2 * x + m, NX * d:NX * d + NX], ACT.Tanh) \
                                .then_inc(S["tanhs"], 1)
                act.wait_ge(S["cells"], s * 2 + (x + 1))
                act.activation(tc[0:TOP, x], c2[0:TOP, x], ACT.Tanh, scale=0.5).then_inc(S["tanh_c"], 1)
                if last:
                    return
                for d, row in ((0, s + 1), (1, s * -1 + (H - 2))):
                    act.wait_ge(S["h2_ready"], s * 4 + (2 * x + d + 1))
                    act.activation(h_rows(xh_hi, row, x), h2[:, x, d].rearrange("p (b w) -> p b w", w=W),
                                   ACT.Copy).then_inc(S["h_hi"], 1)

            for x in range(2):
                step(0, x)
            with act.Fori(1, H - 1) as s:
                for x in range(2):
                    step(s, x)
            for x in range(2):
                step(H - 1, x, last=True)

            for x in range(2):
                act.wait_ge(S[f"hist{x}"], 32 * H)

            def keep(i, b):
                act.wait_ge(S["y_mm"], i + 1)
                act.activation(one_row(y_sb, i), ps[b][:, :], ACT.Copy).then_inc(S["y_kept"], 1)

            with act.Fori(0, H // 4) as j:
                for b in range(2):
                    keep(j * 2 + b, b)
            act.wait_ge(S["stat"], 3)
            act.activation(st[:, 3:4], st[:, 2:3], ACT.Sqrt).then_inc(S["stat"], 1)
            act.wait_ge(S["stat"], 8)

            def relu(i, b):
                act.activation(act_y[:, b], one_row(y_sb, i), ACT.Relu, bias=st[:, 7:8], scale=st[:, 5:6]) \
                    .then_inc(S["relus"], 1)

            relu(0, 0)
            relu(1, 1)
            with act.Fori(1, H // 4) as j:
                for b in range(2):
                    act.wait_ge(S["summed"], j * 2 + b - 1)
                    relu(j * 2 + b, b)

        @block.gpsimd
        def _(pool):
            for t in (xh_hi, xh_lo):
                pool.memset(t[:].bitcast(F32), 0.0).then_inc(S["zeros_set"], 1)
            pool.wait_ge(S["zeros_set"], 2)
            pool.memset(xh_hi[32:HALF].bitcast(F32), 1.0).then_inc(S["zeros_set"], 1)
            pool.wait_ge(S["zeros_set"], 3)
            pool.memset(xh_hi[32:C].bitcast(F32), 0.0).then_inc(S["zeros_set"], 1)
            pool.wait_ge(S["nrows_stored"], 48)
            for b in range(2):
                pool.wait_ge(S[f"y_stored{b}"], 96 * CHUNKS // 2)
            pool.memset(y_hl[32:HALF].bitcast(F32), 0.0).then_inc(S["own_set"], 1)
            pool.memset(y_hl[96:P].bitcast(F32), 1.0).then_inc(S["own_set"], 1)
            pool.memset(xl[32:HALF], 0.0).then_inc(S["own_set"], 1)
            pool.memset(xr[32:HALF], 0.0).then_inc(S["own_set"], 1)
            pool.wait_ge(S["own_set"], 4)

            def unit(g, b, n):
                pool.wait_ge(S[f"x_loaded{b}"], n * 64 + 64)
                pool.tensor_tensor(xr[0:C, b], xl[0:C, b], side[0:C, b], ALU.mult).then_inc(S["xn_ready"], 1)

            def split_ab(g, b, n):
                pool.wait_ge(S["ab_copied"], g * 2 + 2)
                if later(g, 2):
                    pool.wait_ge(S["z_done"], g * 8 - 8)
                    if later(g, 3):
                        pool.wait_ge(S["x1_ready"], g - 2)
                passed(pool, "pool_passed")
                pool.tensor_scalar(ab_hi[:, b], ab[:], 1.0, 0.0, ALU.mult, ALU.add) \
                    .then_inc(S["ab_hi_ready"], 1)
                pool.wait_ge(S["ab_hi_ready"], g + 1)
                pool.tensor_tensor(ab_lo[:, b], ab[:], ab_hi[:, b].bitcast(F32), ALU.subtract) \
                    .then_inc(S["ab_split"], 1)

            def residual(g, b, n):
                if exists(g + 2):
                    pool.wait_ge(S["ab_split"], g + 3)
                pool.wait_ge(S["z2_ready"], g + 1)
                pool.wait_ge(S[f"xres_loaded{b}"], n * 16 + 16)
                if later(n):
                    pool.wait_ge(S[f"x1_stored{b}"], n * 32)
                pool.tensor_tensor(x1[HALF:TOP, b], z2[HALF:TOP], side[HALF:TOP, b], ALU.add) \
                    .then_inc(S["x1_sum"], 1)
                wr = g // PAIRS
                p = g % PAIRS

                def rows(t, h):
                    return t[HALF:TOP, reg(wr * WS, 0, WS), reg(p * (W + 1), h * PAIRS * (W + 1) + 1, W)]

                def part(t, h):
                    return t.rearrange("c (h r w) -> c h r w", h=2, w=W)[:, h]

                for h in range(2):
                    ins = pool.tensor_tensor(rows(xh_hi, h), part(z2[HALF:TOP], h),
                                             part(side[HALF:TOP, b], h), ALU.add)
                ins.then_inc(S["x1_hi"], 1)
                pool.wait_ge(S["x1_sum"], g + 1)
                pool.wait_ge(S["x1_hi"], g + 1)
                for h in range(2):
                    ins = pool.tensor_tensor(rows(xh_lo, h), part(x1[HALF:TOP, b], h),
                                             rows(xh_hi, h).bitcast(F32), ALU.subtract)
                ins.then_inc(S["x1_ready"], 1)

            def turn(j, b):
                for k, stage in ((3, unit), (1, split_ab), (-1, residual)):
                    if exists(nth(j, b, k)[0]):
                        stage(*nth(j, b, k))

            pool.wait_ge(S["zeros_set"], 4)
            unit(0, 0, 0)
            unit(1, 1, 0)
            split_ab(0, 0, 0)
            unit(2, 0, 1)
            turns(pool, turn)
            residual(GROUPS - 1, 1, GROUPS // 2 - 1)

        @block.vector
        def _(dve):
            dve.wait_ge(S["consts0"], 48)
            dve.tensor_tensor(t1[:, 0:1], col1_sb[:, 0:1], col1_sb[:, 1:2], ALU.mult).then_inc(S["t1_ready"], 1)
            dve.wait_ge(S["t1_ready"], 1)
            dve.tensor_tensor(t1[:, 1:2], t1[:, 0:1], col1_sb[:, 2:3], ALU.add).then_inc(S["t1_ready"], 1)
            for c in range(CHUNKS):
                b = c % 2
                dve.wait_ge(S["y_ready"], c + 1)
                if c >= 2:
                    dve.wait_ge(S[f"y_stored{b}"], 96 * (c // 2))
                dve.tensor_copy(y0_hi[:, b], y0[:, b]).then_inc(S["y_hi_ready"], 1)
                dve.wait_ge(S["y_hi_ready"], c + 1)
                dve.tensor_tensor(y0_lo[:, b], y0[:, b], y0_hi[:, b].bitcast(F32), ALU.subtract) \
                    .then_inc(S["y_split"], 1)
            dve.wait_ge(S["nrm_ready"], 1)
            dve.tensor_scalar(nmax[:], nrm[:], 1e-12, None, ALU.max).then_inc(S["norm_parts"], 1)
            dve.tensor_scalar(nunit[:], nrm[:], 1e12, 1.0, ALU.mult, ALU.min).then_inc(S["norm_parts"], 1)
            dve.wait_ge(S["norm_parts"], 2)
            dve.reciprocal(nrows[:, 0], nmax[:]).then_inc(S["nrows_ready"], 1)
            dve.tensor_scalar(nrows[:, 1], nmax[:], -0.5, None, ALU.mult).then_inc(S["nrows_ready"], 1)
            dve.tensor_tensor(nrows[:, 2], nunit[:], nunit[:], ALU.mult).then_inc(S["nrows_ready"], 1)

            dve.wait_ge(S["consts1"], 7 * 16)
            EP = S["edge_parts"]
            dve.tensor_tensor(we[:, 0], we_raw[:, 0], we_raw[:, 1], ALU.subtract).then_inc(EP, 1)
            dve.tensor_tensor(we[:, 1], we_raw[:, 1], we_mul[:], ALU.mult).then_inc(EP, 1)
            dve.tensor_tensor(t2[HALF:TOP, 0:1], col2_sb[HALF:TOP, 0:1], col2_sb[HALF:TOP, 1:2], ALU.mult) \
                .then_inc(EP, 1)
            dve.wait_ge(EP, 3)
            dve.tensor_tensor(we[:, 0], we[:, 0], we_mul[:], ALU.mult).then_inc(EP, 1)
            dve.tensor_tensor(t2[HALF:TOP, 1:2], t2[HALF:TOP, 0:1], col2_sb[HALF:TOP, 2:3], ALU.add) \
                .then_inc(EP, 1)
            dve.wait_ge(EP, 5)
            dve.tensor_tensor(we[:], we[:], we_add[:], ALU.add).then_inc(EP, 1)
            dve.wait_ge(EP, 6)
            for k in range(4):
                dve.tensor_copy(onehot[HALF:P, k // 2, k % 2], ab[HALF:P].rearrange("p w n -> p (w n)")[:, 0:E9])
            dve.tensor_copy(we_hi[:], we[:]).then_inc(S["edge_w"], 1)
            dve.wait_ge(S["edge_w"], 1)
            dve.tensor_tensor(we_lo[:], we[:], we_hi[:].bitcast(F32), ALU.subtract).then_inc(S["edge_w"], 1)

            TP = S["topk_parts"]
            keys_of = [p_keys[:, NODES * t:NODES * t + NODES] for t in range(4)]

            def topk(g, b, n, part):
                if part == 0:
                    dve.wait_ge(S["keys_done"], g + 1)
                    passed(dve, "dve_passed")
                    for t in range(4):
                        ins = dve.max(val8[:, t, 0:8], keys_of[t])
                    ins.then_inc(TP, 1)
                    return
                dve.wait_ge(TP, g * 3 + part)
                if part == 1 and later(n):
                    dve.wait_ge(S[f"idx_stored{b}"], n * 16)
                passed(dve, "dve_passed")
                for t in range(4):
                    if part == 1:
                        dve.max_index(idx[:, b, t, 0:8], val8[:, t, 0:8], keys_of[t])
                        ins = dve.match_replace(keys2[:, t], val8[:, t, 0:8], keys_of[t], LOWEST)
                    elif part == 2:
                        ins = dve.max(val8[:, t, 8:16], keys2[:, t])
                    else:
                        ins = dve.max_index(idx[:, b, t, 8:16], val8[:, t, 8:16], keys2[:, t])
                ins.then_inc(S["topk_done"] if part == 3 else TP, 1)

            def one_hot(g, b, n, q):
                if q == 0:
                    dve.wait_ge(S[f"idx_here{b}"], n * 16 + 16)
                if q >= 2 or later(g):
                    dve.wait_ge(S["z_done"], g * 8 + (2 * q - 2))
                at = HALF * b
                dve.tensor_scalar(onehot[0:HALF, q % 2], ib[at:at + HALF, 2 * q:2 * q + 2],
                                  jcol_sb[at:at + HALF, 0:1], None, ALU.is_equal).then_inc(S["onehots"], 1)

            def maxima(g, b, n, q):
                dve.wait_ge(S["gelus"], g * 8 + (2 * q + 2))
                if q == 0 and later(g, 2):
                    dve.wait_ge(S["fc2_done"], g - 1)
                at = HG * (q // 2) + 2 * WS * (q % 2)
                dst = hmax[:, b, HG * (q // 2):HG * (q // 2) + HG] \
                    .rearrange("p (r w c) -> p w r c", r=WS, c=WS)[:, 2 * (q % 2):2 * (q % 2) + 2]
                dve.tensor_reduce(dst, gel[:, q % 2].rearrange("p w (r c k) -> p w r c k", r=WS, k=K),
                                  AX_X, ALU.max).then_inc(S["maxed"], 1)

            def turn(j, b):
                now, next_ = nth(j, b, 0), nth(j, b, 1)

                def find(part):
                    if exists(nth(j, b, 2)[0]):
                        topk(*nth(j, b, 2), part)

                find(0)
                maxima(*now, 0)
                find(1)
                one_hot(*now, 2)
                find(2)
                maxima(*now, 1)
                one_hot(*now, 3)
                find(3)
                maxima(*now, 2)
                if exists(next_[0]):
                    one_hot(*next_, 0)
                maxima(*now, 3)
                if exists(next_[0]):
                    one_hot(*next_, 1)

            for g in range(2):
                for part in range(4):
                    topk(g, g, 0, part)
            one_hot(0, 0, 0, 0)
            one_hot(0, 0, 0, 1)
            turns(dve, turn)

            for b in range(2):
                dve.wait_ge(S[f"x1_stored{b}"], 32 * (GROUPS // 2))
            dve.wait_ge(S["x1_ready"], GROUPS)
            dve.wait_ge(S["zeros_set"], 4)
            for t in (ti, tf, tg, to, c2, tc):
                dve.memset(t[:], 0.0).then_inc(S["scan_init"], 1)
            dve.wait_ge(S["wl_loaded"], 16)
            n = 0
            for aps in ([wl_raw[:, d, 0] for d in range(2)],
                        [wl_raw[:, d, 1, :, HALF:TOP] for d in range(2)],
                        [wl_raw[0:C, d] for d in range(2)]):
                for part in aps:
                    dve.tensor_scalar(part, part, 0.5, None, ALU.mult).then_inc(S["wl_scaled"], 1)
                    n += 1
                dve.wait_ge(S["wl_scaled"], n)
            dve.tensor_copy(wl_hi[:], wl_raw[:]).then_inc(S["wl_split"], 1)
            dve.wait_ge(S["wl_split"], 1)
            dve.tensor_tensor(wl_lo[:], wl_raw[:], wl_hi[:].bitcast(F32), ALU.subtract) \
                .then_inc(S["wl_split"], 1)
            dve.wait_ge(S["scan_init"], 6)

            def step(s, x, last=False):
                dve.wait_ge(S["tanhs"], s * 16 + (8 * x + 4))
                if later(s):
                    dve.wait_ge(S["cells"], s * 2 + (x - 1))
                dve.scalar_tensor_tensor(cu[0:TOP, x], tf[0:TOP, x], 1.0, c2[0:TOP, x], ALU.add, ALU.mult)
                dve.wait_ge(S["tanhs"], s * 16 + (8 * x + 7))
                dve.scalar_tensor_tensor(cv[0:TOP, x], ti[0:TOP, x], 1.0, tg[0:TOP, x], ALU.add, ALU.mult) \
                    .then_inc(S["cell_parts"], 1)
                dve.wait_ge(S["cell_parts"], s * 2 + (x + 1))
                dve.scalar_tensor_tensor(c2[0:TOP, x], cu[0:TOP, x], 0.5, cv[0:TOP, x], ALU.mult, ALU.add) \
                    .then_inc(S["cells"], 1)
                dve.wait_ge(S["tanh_c"], s * 2 + (x + 1))
                if later(s):
                    dve.wait_ge(S[f"hist{x}"], s * 32)
                for d in range(2):
                    at = HALF * d
                    dve.scalar_tensor_tensor(h2[:, x, d], to[at:at + C, x], 1.0, tc[at:at + C, x],
                                             ALU.add, ALU.mult).then_inc(S["h2_ready"], 1)
                if last:
                    return
                for d, row in ((0, s + 1), (1, s * -1 + (H - 2))):
                    dve.wait_ge(S["h_hi"], s * 4 + (2 * x + d + 1))
                    dve.tensor_tensor(h_rows(xh_lo, row, x), h2[:, x, d].rearrange("p (b w) -> p b w", w=W),
                                      h_rows(xh_hi, row, x).bitcast(F32), ALU.subtract).then_inc(S["h_lo"], 1)

            for x in range(2):
                step(0, x)
            with dve.Fori(1, H - 1) as s:
                for x in range(2):
                    step(s, x)
            for x in range(2):
                step(H - 1, x, last=True)

            dve.wait_ge(S["consts2"], 48)
            dve.tensor_scalar(wp_sb[:], wp_sb[:], 0.5, None, ALU.mult).then_inc(S["wp_ready"], 1)

            def stats(i, b):
                dve.wait_ge(S["y_kept"], i + 1)
                dve.bn_stats(one_row(bst, i), one_row(y_sb, i)).then_inc(S["y_stats"], 1)

            with dve.Fori(0, H // 4) as j:
                for b in range(2):
                    stats(j * 2 + b, b)
            dve.wait_ge(S["y_stats"], H // 2)
            dve.bn_aggr(mv[:, :], bst[:].rearrange("p r n -> p (r n)")).then_inc(S["fold"], 1)
            dve.wait_ge(S["comb_mm"], 1)
            ST = S["stat"]
            dve.tensor_copy(st[:, 0:1], p_comb[:, 4:5]).then_inc(ST, 1)
            dve.wait_ge(ST, 1)
            dve.scalar_tensor_tensor(st[:, 1:2], st[:, 0:1], st[:, 0:1], p_comb[:, 1:2], ALU.mult, ALU.add) \
                .then_inc(ST, 1)
            dve.wait_ge(ST, 2)
            dve.tensor_scalar(st[:, 2:3], st[:, 1:2], EPS, None, ALU.add).then_inc(ST, 1)
            dve.wait_ge(ST, 4)
            dve.reciprocal(st[:, 4:5], st[:, 3:4]).then_inc(ST, 1)
            dve.wait_ge(ST, 5)
            dve.tensor_tensor(st[:, 5:6], st[:, 4:5], gb_sb[:, 0:1], ALU.mult).then_inc(ST, 1)
            dve.wait_ge(ST, 6)
            dve.tensor_tensor(st[:, 6:7], st[:, 5:6], p_comb[:, 0:1], ALU.mult).then_inc(ST, 1)
            dve.wait_ge(ST, 7)
            dve.tensor_tensor(st[:, 7:8], gb_sb[:, 1:2], st[:, 6:7], ALU.subtract).then_inc(ST, 1)

            def add(i, b, n):
                dve.wait_ge(S["relus"], i + 1)
                dve.wait_ge(S[f"x1r{b}"], n * 32 + 32)
                if later(n):
                    dve.wait_ge(S[f"out{b}"], n * 32)
                for h in range(2):
                    at = HALF * h
                    ins = dve.tensor_tensor(fin[at:at + C, b], act_y[at:at + C, b], x1r[at:at + C, b], ALU.add)
                ins.then_inc(S["summed"], 1)

            for b in range(2):
                add(b, b, 0)
            with dve.Fori(1, H // 4) as j:
                for b in range(2):
                    add(j * 2 + b, b, j)


def kernel(**inputs):
    import numpy as np
    import concourse.bacc as bacc
    from concourse.bass_utils import run_bass_kernel_spmd

    f = {k: np.asarray(v) for k, v in inputs.items()}
    z = np.zeros

    def halves(cols):
        t = z((P, cols.shape[1]), np.float32)
        t[0:C] = t[HALF:TOP] = cols
        return t

    x = f["x"].reshape(2, PAIRS, C, WROWS, WS, W // WS, WS)
    xs = z((P, CHUNKS, CHUNK), np.float32)
    by_window = x.transpose(0, 2, 3, 1, 5, 4, 6).reshape(2, C, CHUNKS, CHUNK)
    xs[0:C], xs[HALF:TOP] = by_window[0], by_window[1]
    xrow = x.transpose(2, 3, 1, 0, 4, 5, 6).reshape(C, GROUPS, GN)
    w1 = z((P, P), np.float32)
    w1[0:C, 0:C] = w1[HALF:TOP, HALF:TOP] = f["L0_conv_fc1_w"].T
    ones_sel = z((P, CHUNKS, 2 * CHUNKS), np.float32)
    for c in range(CHUNKS):
        ones_sel[0:C, c, 2 * c] = ones_sel[HALF:TOP, c, 2 * c + 1] = 1.0
    col1 = halves(np.stack([f["L0_conv_fc1_b"], f["L0_conv_fc1_s"], f["L0_conv_fc1_t"]], 1))
    col2 = halves(np.stack([f["L0_conv_fc2_b"], f["L0_conv_fc2_s"], f["L0_conv_fc2_t"]], 1))
    jcol = (np.arange(P, dtype=np.float32) % NODES).reshape(P, 1)
    ewt = f["L0_conv_ew"].T.reshape(2, C, O)
    wedge = z((P, 2, O), np.float32)
    wedge[0:C] = wedge[HALF:TOP] = ewt.transpose(1, 0, 2)
    wedge[TOP, 0] = f["L0_conv_eb"]
    edge_shift = z((P, 2, O), np.float32)
    edge_shift[TOP, 0] = f["L0_conv_et"]
    ident9 = np.repeat(np.eye(NODES, dtype=np.float32), K, axis=1)
    w2 = np.ascontiguousarray(f["L0_conv_fc2_w"].T)
    wl = z((P, 2, 2, TAPS, TOP), np.float32)
    for d, (wn, bn) in enumerate((("L1_conv_w_f", "L1_conv_b_f"), ("L1_conv_w_b", "L1_conv_b_b"))):
        mid = f[wn][:, :, 1, :].reshape(4, C, 2, C, TAPS)
        for gate in range(4):
            m, at = gate // 2, HALF * (gate % 2)
            t = mid[gate].transpose(1, 2, 3, 0)
            wl[HALF:TOP, d, m, :, at:at + C] = t[0]
            wl[0:C, d, m, :, at:at + C] = t[1]
            wl[C, d, m, 1, at:at + C] = f[bn].reshape(4, C)[gate]
    wp = z((O, HALF), np.float32)
    wp[:, 0:C] = f["L1_conv_w_proj"].T
    gb = halves(np.stack([f["L1_conv_gamma"], f["L1_conv_beta"]], 1))
    comb = z((P, 2, P), np.float32)
    for c in range(HALF):
        for q in range(2):
            for r in range(2):
                comb[HALF * q + c, 0, HALF * r + c] = 0.5
                comb[HALF * q + c, 1, HALF * r + c] = 0.5 - q

    arrays = dict(xs=xs, xrow=xrow, w1=w1, ones_sel=ones_sel, col1=col1, jcol=jcol, wedge=wedge,
                  edge_scale=f["L0_conv_es"], edge_shift=edge_shift, ident9=ident9, w2=w2, col2=col2,
                  wl=wl, wp=wp, gb=gb, comb=comb)
    arrays = {k: np.ascontiguousarray(v) for k, v in arrays.items()}
    nc = bacc.Bacc("TRN2", target_bir_lowering=False, num_devices=1)
    aps = {k: nc.dram_tensor(k, v.shape, F32, kind="ExternalInput").ap()
           for k, v in arrays.items()}
    out = nc.dram_tensor("out", (H, C, B, W), F32, kind="ExternalOutput").ap()
    build(nc, **aps, out=out)
    r = run_bass_kernel_spmd(nc, [arrays], core_ids=[0])
    return r.results[0]["out"].transpose(2, 1, 0, 3)
```

```python
from contextlib import ExitStack

import concourse.bass as bass
from concourse import mybir

F32 = mybir.dt.float32
F32R = mybir.dt.float32r
U16 = mybir.dt.uint16
BF16 = mybir.dt.bfloat16
ALU = mybir.AluOpType
ACT = mybir.ActivationFunctionType
AX_X = mybir.AxisListType.X

P = 128
B, C, H, W = 16, 48, 32, 32
O = 2 * C
WS = 8
NODES = WS * WS
K = 9
PAIRS = B // 2
WROWS = H // WS
GROUPS = WROWS * PAIRS
WIN = 2 * (W // WS)
GN = WIN * NODES
HG = GN // 2
CHUNK = 512
CHUNKS = GROUPS * HG // CHUNK
HALF = 64
TOP = HALF + C
E9 = NODES * K
SLOT = (W + 1) * B + 2
TAPS = 3
BX = B // 2
NX = BX * W
EPS = 1e-5
LOWEST = -3.0e38


def split(t):
    return t.rearrange("p (h n) -> p h n", h=2)


def build(nc, xs, xrow, w1, ones_sel, col1, jcol, wedge, edge_scale, edge_shift, ident9, w2, col2,
          wl, wp, gb, comb, out):
    y_d = nc.dram_tensor("y_d", [2, C, 3, GROUPS * HG], F32, kind="Internal").ap()
    nr_d = nc.dram_tensor("nr_d", [3, CHUNKS, 2, 2, HG], F32, kind="Internal").ap()
    idx_d = nc.dram_tensor("idx_d", [GROUPS, WIN, NODES, K], U16, kind="Internal").ap()
    x1_d = nc.dram_tensor("x1_d", [H, C, B, W], F32, kind="Internal").ap()
    hist_d = nc.dram_tensor("hist_d", [H, 2, C, B, W], F32, kind="Internal").ap()

    with ExitStack() as ctx:
        def sem(name):
            return ctx.enter_context(nc.semaphore(name))

        def sb_in(stack):
            return lambda name, shape, dt: stack.enter_context(nc.sbuf_tensor(name, shape, dt))

        sb = sb_in(ctx)
        xh_hi = sb("xh_hi", [P, H, SLOT], F32R)
        with ExitStack() as sx:
            before_middle = sb_in(sx)("before_middle", [P, H // 4, SLOT], F32)
            middle = sb_in(sx)("middle", [P, H // 2, SLOT], F32)
        x1r = middle[:, :, 0:B * W]
        xh_lo = sb("xh_lo", [P, H, SLOT], F32R)

        with ExitStack() as s01:
            a = sb_in(s01)
            jcol_sb = a("jcol_sb", [P, 1], F32)
            we_raw = a("we_raw", [P, 2, O], F32)
            we_mul = a("we_mul", [P, O], F32)
            we_add = a("we_add", [P, 2, O], F32)
            we = a("we", [P, 2, O], F32)
            we_hi = a("we_hi", [P, 2, O], F32R)
            we_lo = a("we_lo", [P, 2, O], F32R)
            w2_sb = a("w2_sb", [O, C], F32)
            col2_sb = a("col2_sb", [P, 3], F32)
            t2 = a("t2", [P, 2], F32)

            with ExitStack() as s0:
                a = sb_in(s0)
                x_in = a("x_in", [P, CHUNKS, CHUNK], F32)
                w1_sb = a("w1_sb", [P, P], F32)
                sel_sb = a("sel_sb", [P, CHUNKS, 2 * CHUNKS], F32)
                col1_sb = a("col1_sb", [P, 3], F32)
                t1 = a("t1", [P, 2], F32)
                t1_root = a("t1_root", [P, 1], F32)
                y3 = a("y3", [P, 3, 3, CHUNK], F32R)
                y_sq = a("y_sq", [P, 3, CHUNK], F32)
                nrm = a("nrm", [2 * CHUNKS, CHUNK], F32)
                nmax = a("nmax", [2 * CHUNKS, CHUNK], F32)
                nunit = a("nunit", [2 * CHUNKS, CHUNK], F32)
                nrows = a("nrows", [2 * CHUNKS, 3, CHUNK], F32)

            with ExitStack() as s1:
                a = sb_in(s1)
                y_hl = a("y_hl", [P, 2, GN], F32R)
                xl = a("xl", [P, 2, GN], F32)
                xr = a("xr", [P, 2, GN], F32)
                onehot = a("onehot", [P, 2, WIN // 2, E9], BF16)
                ab = a("ab", [P, WIN, O], F32)
                keys2 = a("keys2", [P, 4, NODES], F32)
                val8 = a("val8", [P, 4, 16], F32)
                idx = a("idx", [P, 2, 4, 16], U16)
                ib = a("ib", [P, WIN, E9], U16)
                gel = a("gel", [O, 2, 2, E9], F32)
                hmax = a("hmax", [O, 2, GN], F32)
                ab3 = a("ab3", [P, 3, 2, WIN, O], BF16)
                side = a("side", [P, 2, GN], F32)
                z2 = a("z2", [P, GN], F32)
                x1 = a("x1", [P, 2, GN], F32)

        with ExitStack() as s2:
            a = sb_in(s2)
            wp_sb = a("wp_sb", [O, HALF], F32)
            gb_sb = a("gb_sb", [P, 2], F32)
            comb_sb = a("comb_sb", [P, 2, P], F32)
            bst = a("bst", [P, H // 2, 6], F32)
            mv = a("mv", [P, 2], F32)
            st = a("st", [P, 8], F32)
            h2 = a("h2", [C, 2, 2, NX], F32)
            wl_hi = a("wl_hi", [P, 2, 2, TAPS, TOP], F32R)
            with ExitStack() as s2w:
                wl_raw = sb_in(s2w)("wl_raw", [P, 2, 2, TAPS, TOP], F32)
            wl_lo = a("wl_lo", [P, 2, 2, TAPS, TOP], F32R)
            ti = a("ti", [P, 2, NX], F32)
            tf = a("tf", [P, 2, NX], F32)
            tg = a("tg", [P, 2, NX], F32)
            to = a("to", [P, 2, NX], F32)
            cu = a("cu", [P, 2, NX], F32)
            cv = a("cv", [P, 2, NX], F32)
            c2 = a("c2", [P, 2, NX], F32)
            tc = a("tc", [P, 2, NX], F32)
            hp = a("hp", [O, 2, 2, B * W], F32)
            y_sb = a("y_sb", [P, H // 2, B * W], F32)

        pz = ctx.enter_context(nc.psum_tensor("pz", [P, 4, 512], F32))
        ps = [ctx.enter_context(nc.psum_tensor(f"ps{i}", [P, 512], F32)) for i in range(4)]
        p_fc1 = (ps[0], ps[1], ps[3])
        p_nrm = ps[2]
        p_keys = ps[0]
        p_ab = ps[1:3]
        p_fc2 = ps[3]
        p_comb = ps[2]

        names = """consts0 consts1 x_in0 x_in1 x_in2 t1_ready table_here fc1_done y_ready y_sq_ready nrm_done
            y_hi_ready y_split y_stored0 y_stored1 y_stored2 nrm_ready norm_parts nrows_ready nrows_stored
            zeros_set pads_set own_loaded edge_parts edge_w own_set
            y_loaded0 y_loaded1 x_loaded0 x_loaded1 xres_loaded0 xres_loaded1 xn_ready keys_done
            topk_parts topk_done idx_stored0 idx_stored1 idx_here0 idx_here1 onehots ab_mm ab_copied
            ab_part ab_rest ab_split z_done gelus maxed fc2_done z2_ready x1_sum x1_hi x1_split
            x1_stored0 x1_stored1 sp_passed pool_passed dve_passed
            wl_loaded wl_scaled wl_split scan_init gates tanh_if tanh_go cells cell_parts tanh_c
            h2_ready h_hi h_lo hist0 hist1 consts2 wp_ready hp_loaded0 hp_loaded1 y_mm y_kept y_stats
            fold comb_mm stat x1r_pads x1r_loaded relus summed outs""".split()
        S = {n: sem(n) for n in names}
        block = ctx.enter_context(nc.Block())

        def reg(v, lo, n):
            return slice(v + lo, v + lo + n) if isinstance(v, int) else bass.ds(v + lo, n)

        def later(v, n=1):
            return not isinstance(v, int) or v >= n

        def nth(j, b, k):
            return j * 2 + (b + k), (b + k) % 2, j + (b + k) // 2

        def exists(g):
            return not isinstance(g, int) or 0 <= g < GROUPS

        def turns(engine, turn):
            for b in range(2):
                turn(0, b)
            with engine.Fori(1, GROUPS // 2 - 2) as j:
                for b in range(2):
                    turn(j, b)
            for j in (GROUPS // 2 - 2, GROUPS // 2 - 1):
                for b in range(2):
                    turn(j, b)

        def passed(engine, name):
            engine.sem_inc(S[name], 1)

        def one_row(t, i):
            return t[:, reg(i, 0, 1)].rearrange("p o n -> p (o n)")

        def chunks(engine, chunk):
            def three(j):
                for k in (1, 2, 3):
                    chunk(j * 3 + k, k % 3, j + k // 3)
            chunk(0, 0, 0)
            three(0)
            with engine.Fori(1, CHUNKS // 3 - 1) as j:
                three(j)
            three(CHUNKS // 3 - 1)

        def slots(t, g):
            wr, p = g // PAIRS, g % PAIRS
            return t[HALF:TOP, reg(wr * WS, 0, WS), 0:(W + 1) * B] \
                .rearrange("c r (h n) -> c h r n", h=2)[:, :, :, reg(p * (W + 1), 1, W)]

        def by_row(t):
            return t.rearrange("c (h r w) -> c h r w", h=2, w=W)

        def h_rows(t, row, x):
            at = (W + 1) * BX * x + 1
            return t[0:C, reg(row, 0, 1), at:at + (W + 1) * BX] \
                .rearrange("p o (b w) -> p (o b) w", w=W + 1)[:, :, 0:W]

        @block.sync
        def _(sp):
            parts = (0, 1, 4, CHUNKS)
            sp.dma_start(w1_sb[:], w1).then_inc(S["consts0"], 16)
            for k in range(3):
                sp.dma_start(x_in[0:TOP, parts[k]:parts[k + 1]], xs[:, parts[k]:parts[k + 1]]) \
                    .then_inc(S[f"x_in{k}"], 16)
                if k == 0:
                    sp.dma_start(col1_sb[:], col1).then_inc(S["consts0"], 16)
                    sp.dma_start(sel_sb[:], ones_sel).then_inc(S["consts0"], 16)
            sp.dma_start(jcol_sb[:], jcol).then_inc(S["consts1"], 16)
            sp.dma_start(we_raw[:], wedge).then_inc(S["consts1"], 16)
            sp.dma_start(we_mul[:], edge_scale.rearrange("(o n) -> o n", o=1).to_broadcast([P, O])) \
                .then_inc(S["consts1"], 16)
            sp.dma_start(we_add[:], edge_shift).then_inc(S["consts1"], 16)
            sp.dma_start(w2_sb[:], w2).then_inc(S["consts1"], 16)
            sp.dma_start(col2_sb[:], col2).then_inc(S["consts1"], 16)

            def store_y(c, b, n):
                sp.wait_ge(S["y_split"], c + 1)
                for h in range(2):
                    sp.dma_start(y_d[h, :, :, reg(c * CHUNK, 0, CHUNK)],
                                 y3[HALF * h:HALF * h + C, b].bitcast(F32)).then_inc(S[f"y_stored{b}"], 16)

            chunks(sp, store_y)
            sp.wait_ge(S["fc1_done"], CHUNKS)
            sp.dma_start(ab[HALF:P].rearrange("p w n -> p (w n)")[:, 0:E9], ident9).then_inc(S["own_loaded"], 16)
            for b, uses in enumerate((6, 5, 5)):
                sp.wait_ge(S[f"y_stored{b}"], 32 * uses)
            sp.wait_ge(S["pads_set"], 4)

            def load_y(g, b, n):
                if later(g, 2):
                    sp.wait_ge(S["ab_mm"], g * 2 - 2)
                for form, at in ((1, 0), (2, HALF)):
                    sp.dma_start(split(y_hl[at:at + C, b].bitcast(F32)),
                                 y_d[:, :, form, reg(g * HG, 0, HG)].rearrange("h c n -> c h n")) \
                        .then_inc(S[f"y_loaded{b}"], 16)

            def load_whole(g, b):
                sp.dma_start(split(xl[0:C, b]), y_d[:, :, 0, reg(g * HG, 0, HG)].rearrange("h c n -> c h n")) \
                    .then_inc(S[f"x_loaded{b}"], 16)

            def load_norms(b, n):
                for q, dst in ((0, side[0:C, b]), (1, xl[HALF:HALF + 1, b]), (2, xr[HALF:HALF + 1, b])):
                    src = nr_d[q, reg(n, 0, 1), :, b]
                    if q == 0:
                        src = src.to_broadcast([C, 2, HG])
                    sp.dma_start(split(dst), src).then_inc(S[f"x_loaded{b}"], 16)

            def load_x(g, b, n):
                sp.wait_ge(S["keys_done"], g - 1)
                load_whole(g, b)
                load_norms(b, n)

            def load_xres(g, b, n):
                sp.dma_start(side[HALF:TOP, b], xrow[:, reg(g, 0, 1)].rearrange("c o n -> c (o n)")) \
                    .then_inc(S[f"xres_loaded{b}"], 16)

            def pass_idx(g, b, n):
                sp.wait_ge(S["topk_done"], g + 1)
                sp.dma_start(idx_d[reg(g, 0, 1)].rearrange("o (t s) n k -> (o s n) t k", s=2),
                             idx[:, b, :, 0:K]).then_inc(S[f"idx_stored{b}"], 16)
                sp.wait_ge(S[f"idx_stored{b}"], n * 16 + 16)
                sp.dma_start(ib[HALF * b:HALF * b + HALF],
                             idx_d[reg(g, 0, 1)].rearrange("o w n k -> o w (n k)")
                             .to_broadcast([HALF, WIN, E9])).then_inc(S[f"idx_here{b}"], 16)

            def store_x1(g, b, n):
                sp.wait_ge(S["x1_sum"], g + 1)
                wr = g // PAIRS
                p = g % PAIRS
                for h in range(2):
                    dst = x1_d[reg(wr * WS, 0, WS), :, reg(p, h * PAIRS, 1)]
                    sp.dma_start(dst.rearrange("r c o w -> c (r o) w"),
                                 x1[HALF:TOP, b].rearrange("c (h r w) -> c h r w", h=2, w=W)[:, h]) \
                        .then_inc(S[f"x1_stored{b}"], 16)

            load_whole(0, 0)
            load_y(0, 0, 0)
            sp.wait_ge(S["nrows_ready"], 3)
            sp.dma_start(nr_d.rearrange("q c h g n -> (c h) q (g n)"), nrows[:]).then_inc(S["nrows_stored"], 16)
            load_whole(1, 1)
            load_y(1, 1, 0)
            sp.wait_ge(S["nrows_stored"], 16)
            for g in range(2):
                load_norms(g, 0)
            load_xres(0, 0, 0)
            load_x(2, 0, 1)
            load_y(2, 0, 1)
            pass_idx(0, 0, 0)
            load_x(3, 1, 1)
            pass_idx(1, 1, 0)

            def load_scan_weights():
                sp.wait_ge(S["ab_mm"], 2 * GROUPS)
                sp.wait_ge(S["keys_done"], GROUPS)
                sp.dma_start(wl_raw[:], wl).then_inc(S["wl_loaded"], 16)

            def turn(j, b):
                if isinstance(j, int) and nth(j, b, 0)[0] == GROUPS - 1:
                    load_scan_weights()
                for k, stage in ((4, load_x), (3, load_y), (2, pass_idx), (-1, store_x1), (1, load_xres)):
                    if exists(nth(j, b, k)[0]):
                        stage(*nth(j, b, k))

            turns(sp, turn)
            store_x1(GROUPS - 1, 1, GROUPS // 2 - 1)
            for b in range(2):
                sp.wait_ge(S[f"x1_stored{b}"], 32 * (GROUPS // 2))

            sp.dma_start(wp_sb[:], wp).then_inc(S["consts2"], 16)
            sp.dma_start(gb_sb[:], gb).then_inc(S["consts2"], 16)
            sp.dma_start(comb_sb[:], comb).then_inc(S["consts2"], 16)

            def store_h(s, x):
                sp.wait_ge(S["h2_ready"], s * 4 + (2 * x + 2))
                for d, row in ((0, s), (1, s * -1 + (H - 1))):
                    dst = hist_d[reg(row, 0, 1), d, :, BX * x:BX * x + BX].rearrange("o c b w -> (o c) (b w)")
                    sp.dma_start(dst, h2[:, x, d]).then_inc(S[f"hist{x}"], 16)

            def load_h(s, b):
                for x in range(2):
                    sp.wait_ge(S[f"hist{x}"], s * 32 + 32)
                    passed(sp, "sp_passed")
                if later(s, H // 2 + 2):
                    sp.wait_ge(S["y_mm"], s - (H // 2 + 1))
                for q, row in ((0, s), (1, s * -1 + (H - 1))):
                    sp.dma_start(hp[:, b, q], hist_d[reg(row, 0, 1)].rearrange("o d c b w -> (o d c) (b w)")) \
                        .then_inc(S[f"hp_loaded{b}"], 16)

            def step(s, b):
                for x in range(2):
                    store_h(s, x)
                if later(s, H // 2 + 1):
                    load_h(s - 1, 1 - b)

            step(0, 0)
            with sp.Fori(0, H // 4) as j:
                for b in range(2):
                    for x in range(2):
                        store_h(j * 2 + (1 + b), x)
            step(17, 1)
            with sp.Fori(0, H // 4 - 4) as j:
                for b in range(2):
                    step(j * 2 + (18 + b), b)
            sp.wait_ge(S["x1r_pads"], 1)
            with sp.Fori(0, 2) as j:
                for b in range(2):
                    i = j * 8 + 4 * b
                    sp.dma_start(x1r[0:C, reg(i, 0, 4)], x1_d[reg(i, H // 2, 4)].rearrange("r c b w -> c r (b w)")) \
                        .then_inc(S["x1r_loaded"], 16)
                    for k in range(4):
                        sp.dma_start(x1r[HALF:TOP, reg(i, k, 1)],
                                     x1_d[reg(i * -1, H // 2 - 1 - k, 1)].rearrange("r c b w -> c r (b w)")) \
                            .then_inc(S["x1r_loaded"], 16)
                    step(j * 2 + (26 + b), b)
            step(30, 0)
            step(31, 1)
            load_h(31, 1)

            with sp.Fori(0, H // 8) as j:
                sp.wait_ge(S["summed"], j * 4 + 4)
                for q in range(2):
                    sp.dma_start(out[q, :, reg(j * 4, 0, 4)], y_sb[HALF * q:HALF * q + C, reg(j * 4, 0, 4)]) \
                        .then_inc(S["outs"], 16)
            sp.wait_ge(S["outs"], 32 * H // 8)

        @block.tensor
        def _(pe):
            pe.wait_ge(S["consts0"], 48)

            def norms(c, b, first=False, last=False):
                pe.wait_ge(S["y_sq_ready"], c + 1)
                pe.matmul(p_nrm[0:2 * CHUNKS, :], sel_sb[:, c], y_sq[:, b], start=first, stop=last) \
                    .then_inc(S["nrm_done"], 1)

            def chunk(c, b, n):
                if c in (1, 3):
                    pe.wait_ge(S[f"x_in{1 + c // 3}"], 16)
                if later(n):
                    pe.wait_ge(S["y_sq_ready"], c - 2)
                pe.matmul(p_fc1[b][:, :], w1_sb[0:TOP, :], one_row(x_in, c)[0:TOP], start=True, stop=True) \
                    .then_inc(S["fc1_done"], 1)
                if later(c):
                    norms(c - 1, (b - 1) % 3, first=(c == 1))

            pe.wait_ge(S["x_in0"], 16)
            for c in range(CHUNKS):
                chunk(c, c % 3, c // 3)
            norms(CHUNKS - 1, (CHUNKS - 1) % 3, last=True)

            pe.wait_ge(S["edge_w"], 2)
            pe.wait_ge(S["nrm_ready"], 1)

            def keys(g, b, n):
                pe.wait_ge(S["xn_ready"], g + 1)
                if later(g):
                    pe.wait_ge(S["topk_parts"], g * 3 - 1)
                for w in range(WIN):
                    lo, at = NODES * w, NODES * (w // 2)
                    mm = pe.matmul(p_keys[HALF * (w % 2):HALF * (w % 2) + HALF, at:at + NODES],
                                   xl[0:HALF + 1, b, lo:lo + NODES], xr[0:HALF + 1, b, lo:lo + NODES],
                                   start=True, stop=True)
                mm.then_inc(S["keys_done"], 1)

            def edges(g, b, n):
                pe.wait_ge(S[f"y_loaded{b}"], n * 32 + 32)
                for k in range(2):
                    if later(g):
                        pe.wait_ge(S["ab_copied"], g * 2 + (k - 1))
                    for q in range(2):
                        at = 2 * NODES * (2 * k + q)
                        lhs = y_hl[:, b, at:at + 2 * NODES]
                        o = p_ab[k][:, 2 * O * q:2 * O * q + 2 * O]
                        pe.matmul(o, lhs, we_hi[:].rearrange("p a o -> p (a o)"), start=True, stop=False)
                        mm = pe.matmul(o, lhs, we_lo[:].rearrange("p a o -> p (a o)"), start=False, stop=True)
                    mm.then_inc(S["ab_mm"], 1)

            def gather(g, q, b):
                if q == 0:
                    pe.wait_ge(S["ab_split"], g + 1)
                pe.wait_ge(S["onehots"], g * 2 + (q // 2 + 1))
                for s in range(2):
                    w = 2 * q + s
                    if q > 0 or later(g):
                        pe.wait_ge(S["gelus"], g * 8 + (w - 1))
                    for h in range(2):
                        o = pz[0:O, 2 * s + h, 0:E9 // 2]
                        rhs = onehot[:, q // 2, 2 * (q % 2) + s, h * (E9 // 2):(h + 1) * (E9 // 2)]
                        for part in range(3):
                            mm = pe.matmul(o, ab3[:, part, b, w], rhs, start=(part == 0), stop=(part == 2))
                    mm.then_inc(S["z_done"], 1)

            def fc2(g, b, n):
                pe.wait_ge(S["maxed"], g * 4 + 4)
                if later(g):
                    pe.wait_ge(S["z2_ready"], g)
                pe.matmul(p_fc2[HALF:TOP, :], w2_sb[:, :], hmax[:, b], start=True, stop=True) \
                    .then_inc(S["fc2_done"], 1)

            def turn(j, b):
                def gathers(*which):
                    for k, q in which:
                        g, buf, _ = nth(j, b, k)
                        if exists(g):
                            gather(g, q, buf)

                gathers((0, 2))
                if exists(nth(j, b, -1)[0]):
                    fc2(*nth(j, b, -1))
                gathers((0, 3))
                for k, stage in ((2, edges), (3, keys)):
                    if exists(nth(j, b, k)[0]):
                        stage(*nth(j, b, k))
                gathers((1, 0), (1, 1))

            keys(0, 0, 0)
            edges(0, 0, 0)
            keys(1, 1, 0)
            edges(1, 1, 0)
            gather(0, 0, 0)
            keys(2, 0, 1)
            gather(0, 1, 0)
            turns(pe, turn)
            fc2(GROUPS - 1, 1, GROUPS // 2 - 1)

            pe.wait_ge(S["x1_split"], GROUPS)
            pe.wait_ge(S["wl_split"], 2)

            def gates(s, x):
                for m in range(2):
                    if later(s):
                        pe.wait_ge(S["tanh_go" if m else "tanh_if"], s * 8 + (4 * x - 4))
                    for d in range(2):
                        if m == 0 and later(s):
                            pe.wait_ge(S["h_hi"], s * 4 + (2 * x + d - 3))
                        row = s if d == 0 else s * -1 + (H - 1)
                        o = pz[0:TOP, 2 * x + m, NX * d:NX * d + NX]
                        n = 0
                        for src, wgt in ((xh_hi, wl_hi), (xh_hi, wl_lo), (xh_lo, wl_hi)):
                            if n == 6 and m == 0 and later(s):
                                pe.wait_ge(S["h_lo"], s * 4 + (2 * x + d - 3))
                            for t in range(TAPS):
                                at = (W + 1) * BX * x + t
                                rhs = src[0:TOP, reg(row, 0, 1), at:at + (W + 1) * BX] \
                                    .rearrange("p o (b w) -> p (o b) w", w=W + 1)[:, :, 0:W]
                                mm = pe.matmul(o, wgt[0:TOP, d, m, t], rhs, start=(n == 0), stop=(n == 8))
                                n += 1
                    mm.then_inc(S["gates"], 1)

            def project(i, b, n):
                pe.wait_ge(S[f"hp_loaded{b}"], n * 32 + 32)
                if later(i, 2):
                    pe.wait_ge(S["y_kept"], i - 1)
                for q in range(2):
                    mm = pe.matmul(ps[b][HALF * q:HALF * q + HALF, :], wp_sb[:, :], hp[:, b, q],
                                   start=True, stop=True)
                mm.then_inc(S["y_mm"], 1)

            def step(s, b):
                for x in range(2):
                    gates(s, x)
                if later(s, H // 2 + 2):
                    project(s - (H // 2 + 2), b, (s - (H // 2 + 2)) // 2)

            step(0, 0)
            with pe.Fori(0, H // 4) as j:
                for b in range(2):
                    for x in range(2):
                        gates(j * 2 + (1 + b), x)
            step(17, 1)
            pe.wait_ge(S["wp_ready"], 1)
            step(18, 0)
            step(19, 1)
            with pe.Fori(1, H // 4 - 2) as j:
                for b in range(2):
                    for x in range(2):
                        gates(j * 2 + (18 + b), x)
                    project(j * 2 + b, b, j)
            step(30, 0)
            step(31, 1)
            project(14, 0, 7)
            project(15, 1, 7)
            pe.wait_ge(S["fold"], 1)
            for q in range(2):
                mm = pe.matmul(p_comb[:, 4 * q:4 * q + 2], comb_sb[:, q], mv[:, :], start=True, stop=True)
            mm.then_inc(S["comb_mm"], 1)

        @block.scalar
        def _(act):
            act.wait_ge(S["t1_ready"], 2)
            act.activation(t1_root[:], col1_sb[:, 1:2], ACT.Sqrt, scale=0.0).then_inc(S["table_here"], 1)

            def chunk(c, b, n):
                act.wait_ge(S["fc1_done"], c + 1)
                if later(n):
                    act.wait_ge(S[f"y_stored{b}"], n * 32)
                    act.wait_ge(S["nrm_done"], c - 2)
                act.activation(y3[:, b, 0].bitcast(F32), p_fc1[b][:, :], ACT.Identity, bias=t1[:, 1:2],
                               scale=col1_sb[:, 1:2]).then_inc(S["y_ready"], 1)
                act.activation(y_sq[:, b], p_fc1[b][:, :], ACT.Square, bias=t1[:, 1:2],
                               scale=col1_sb[:, 1:2]).then_inc(S["y_sq_ready"], 1)

            chunks(act, chunk)
            act.wait_ge(S["nrm_done"], CHUNKS)
            act.activation(nrm[:], p_nrm[0:2 * CHUNKS, :], ACT.Sqrt).then_inc(S["nrm_ready"], 1)

            act.wait_ge(S["edge_w"], 2)
            act.wait_ge(S["nrows_stored"], 16)

            def copy_ab(g, b):
                for k in range(2):
                    act.wait_ge(S["ab_mm"], g * 2 + (k + 1))
                    if k == 0 and later(g):
                        act.wait_ge(S["ab_split"], g)
                    bank = p_ab[k][:, 0:4 * O].rearrange("p (q a o) -> p q a o", q=2, a=2)
                    to_windows = ab[:, 4 * k:4 * k + 4].rearrange("p (q s) o -> p q s o", s=2)
                    for s in range(2):
                        rows = slice(HALF * s, HALF * s + HALF)
                        act.activation(to_windows[0:HALF, :, s], bank[rows, :, 1], ACT.Copy)
                        ins = act.activation(to_windows[HALF:P, :, s], bank[rows, :, 0], ACT.Copy)
                    ins.then_inc(S["ab_copied"], 1)
                act.wait_ge(S["ab_copied"], g * 2 + 2)
                if later(g, 2):
                    act.wait_ge(S["z_done"], g * 8 - 8)
                act.activation(ab3[:, 0, b], ab[:], ACT.Copy).then_inc(S["ab_part"], 1)

            def gelu(g, q):
                for s in range(2):
                    act.wait_ge(S["z_done"], g * 8 + (2 * q + s + 1))
                    if q >= 2 or later(g):
                        act.wait_ge(S["maxed"], g * 4 + (q - 1))
                    act.activation(gel[:, q % 2, s].rearrange("p (h n) -> p h n", h=2),
                                   pz[0:O, 2 * s:2 * s + 2, 0:E9 // 2], ACT.Gelu).then_inc(S["gelus"], 1)

            def fc2_out(g):
                act.wait_ge(S["fc2_done"], g + 1)
                if later(g):
                    act.wait_ge(S["x1_sum"], g)
                act.activation(z2[HALF:TOP], p_fc2[HALF:TOP, :], ACT.Identity, bias=t2[HALF:TOP, 1:2],
                               scale=col2_sb[HALF:TOP, 1:2]).then_inc(S["z2_ready"], 1)

            def x1_high(g, b):
                act.wait_ge(S["x1_sum"], g + 1)
                act.activation(slots(xh_hi, g), by_row(x1[HALF:TOP, b]), ACT.Copy).then_inc(S["x1_hi"], 1)

            def turn(j, b):
                (g, _, _), next_, last = nth(j, b, 0), nth(j, b, 1), nth(j, b, -1)
                gelu(g, 1)
                gelu(g, 2)
                if exists(last[0]):
                    fc2_out(last[0])
                if exists(g - 2):
                    x1_high(*nth(j, b, -2)[0:2])
                gelu(g, 3)
                if exists(g + 2):
                    copy_ab(*nth(j, b, 2)[0:2])
                if exists(next_[0]):
                    gelu(next_[0], 0)

            act.wait_ge(S["own_set"], WIN)
            act.wait_ge(S["zeros_set"], 10)
            copy_ab(0, 0)
            gelu(0, 0)
            copy_ab(1, 1)
            turns(act, turn)
            x1_high(GROUPS - 2, 0)
            fc2_out(GROUPS - 1)
            x1_high(GROUPS - 1, 1)

            act.wait_ge(S["scan_init"], 4)

            def tanh_gate(s, x, m, d, dst, at):
                act.activation(dst[HALF * d:HALF * d + C, x],
                               pz[at:at + C, 2 * x + m, NX * d:NX * d + NX], ACT.Tanh) \
                    .then_inc(S["tanh_go" if m else "tanh_if"], 1)

            def gate_i(s, x):
                act.wait_ge(S["gates"], s * 4 + (2 * x + 1))
                if later(s):
                    act.wait_ge(S["cell_parts"], s * 2 + (x - 1))
                for d in range(2):
                    tanh_gate(s, x, 0, d, ti, 0)

            def gate_f(s, x):
                for d in range(2):
                    tanh_gate(s, x, 0, d, tf, HALF)

            def gates_g_o(s, x):
                act.wait_ge(S["gates"], s * 4 + (2 * x + 2))
                if later(s):
                    act.wait_ge(S["h2_ready"], s * 4 + (2 * x - 2))
                for d in range(2):
                    tanh_gate(s, x, 1, d, tg, 0)
                for d in range(2):
                    tanh_gate(s, x, 1, d, to, HALF)

            def keep(i, b):
                act.wait_ge(S["y_mm"], i + 1)
                act.activation(one_row(y_sb, i), ps[b][:, :], ACT.Copy).then_inc(S["y_kept"], 1)

            def step(s, b, projects=False):
                for x in range(2):
                    gates_g_o(s, x)
                    act.wait_ge(S["cells"], s * 2 + (x + 1))
                    act.activation(tc[0:TOP, x], c2[0:TOP, x], ACT.Tanh, scale=0.5).then_inc(S["tanh_c"], 1)
                    more = x == 0 or not (isinstance(s, int) and s == H - 1)
                    following = (s, 1) if x == 0 else (s + 1, 0)
                    if more:
                        gate_i(*following)
                    for d, row in ((0, s + 1), (1, s * -1 + (H - 2))):
                        if isinstance(s, int) and s == H - 1:
                            break
                        act.wait_ge(S["h2_ready"], s * 4 + (2 * x + d + 1))
                        act.activation(h_rows(xh_hi, row, x), h2[:, x, d].rearrange("p (b w) -> p b w", w=W),
                                       ACT.Copy).then_inc(S["h_hi"], 1)
                    if more:
                        gate_f(*following)
                    if x == 0 and projects:
                        keep(s - (H // 2 + 3), 1 - b)

            gate_i(0, 0)
            gate_f(0, 0)
            step(0, 0)
            with act.Fori(0, H // 4) as j:
                for b in range(2):
                    step(j * 2 + (1 + b), 1 - b)
            step(17, 1)
            step(18, 0)
            step(19, 1, projects=True)
            with act.Fori(1, H // 4 - 2) as j:
                for b in range(2):
                    step(j * 2 + (18 + b), b, projects=True)
            step(30, 0, projects=True)
            step(31, 1, projects=True)

            for i in range(13, H // 2):
                keep(i, i % 2)
            act.wait_ge(S["stat"], 3)
            act.activation(st[:, 3:4], st[:, 2:3], ACT.Sqrt).then_inc(S["stat"], 1)
            act.wait_ge(S["stat"], 8)

            with act.Fori(0, H // 2) as i:
                act.activation(one_row(y_sb, i), one_row(y_sb, i), ACT.Relu, bias=st[:, 7:8],
                               scale=st[:, 5:6]).then_inc(S["relus"], 1)

        @block.gpsimd
        def _(pool):
            pool.memset(xh_hi[32:HALF].bitcast(F32), 1.0).then_inc(S["zeros_set"], 1)
            pool.memset(xh_lo[32:HALF].bitcast(F32), 0.0).then_inc(S["zeros_set"], 1)
            pool.wait_ge(S["zeros_set"], 2)
            for t in (xh_hi, xh_lo):
                pool.memset(t[0:HALF, :, 0:(W + 1) * B + 1:W + 1].bitcast(F32), 0.0).then_inc(S["zeros_set"], 1)
                pool.memset(t[HALF:P, :, 0:(W + 1) * B + 1:W + 1].bitcast(F32), 0.0).then_inc(S["zeros_set"], 1)
            pool.wait_ge(S["zeros_set"], 6)
            for t in (xh_hi, xh_lo):
                for row in (0, H - 1):
                    pool.memset(t[0:C, row].bitcast(F32), 0.0).then_inc(S["zeros_set"], 1)
            pool.wait_ge(S["zeros_set"], 10)
            pool.wait_ge(S["fc1_done"], CHUNKS)
            pool.memset(y_hl[32:HALF].bitcast(F32), 0.0).then_inc(S["pads_set"], 1)
            pool.memset(y_hl[96:P].bitcast(F32), 1.0).then_inc(S["pads_set"], 1)
            pool.memset(xl[32:HALF], 0.0).then_inc(S["pads_set"], 1)
            pool.memset(xr[32:HALF], 0.0).then_inc(S["pads_set"], 1)
            pool.wait_ge(S["pads_set"], 4)
            pool.wait_ge(S["zeros_set"], 10)

            def unit(g, b, n):
                pool.wait_ge(S[f"x_loaded{b}"], n * 64 + 64)
                pool.tensor_tensor(xr[0:C, b], xl[0:C, b], side[0:C, b], ALU.mult) \
                    .then_inc(S["xn_ready"], 1)

            def split_ab(g, b, n):
                if later(g, 3):
                    pool.wait_ge(S["x1_sum"], g - 2)
                pool.wait_ge(S["ab_part"], g + 1)
                pool.tensor_tensor(ab[:], ab[:], ab3[:, 0, b], ALU.subtract).then_inc(S["ab_rest"], 1)
                pool.wait_ge(S["ab_rest"], g * 2 + 1)
                passed(pool, "pool_passed")
                pool.tensor_scalar(ab3[:, 1, b], ab[:], 1.0, 0.0, ALU.mult, ALU.add).then_inc(S["ab_rest"], 1)
                pool.wait_ge(S["ab_rest"], g * 2 + 2)
                pool.tensor_tensor(ab3[:, 2, b], ab[:], ab3[:, 1, b], ALU.subtract).then_inc(S["ab_split"], 1)


            def residual(g, b, n):
                if isinstance(g, int) and g < 2:
                    pool.wait_ge(S["ab_split"], g + 3)
                pool.wait_ge(S["z2_ready"], g + 1)
                pool.wait_ge(S[f"xres_loaded{b}"], n * 16 + 16)
                if later(n):
                    pool.wait_ge(S[f"x1_stored{b}"], n * 32)
                pool.tensor_tensor(x1[HALF:TOP, b], z2[HALF:TOP], side[HALF:TOP, b], ALU.add) \
                    .then_inc(S["x1_sum"], 1)

            def x1_low(g, b, n):
                if exists(g + 3):
                    pool.wait_ge(S["ab_split"], g + 4)
                pool.wait_ge(S["x1_hi"], g + 1)
                pool.tensor_tensor(slots(xh_lo, g), by_row(x1[HALF:TOP, b]), slots(xh_hi, g).bitcast(F32),
                                   ALU.subtract).then_inc(S["x1_split"], 1)

            def turn(j, b):
                for k, stage in ((3, unit), (-2, x1_low), (-1, residual), (2, split_ab)):
                    if exists(nth(j, b, k)[0]):
                        stage(*nth(j, b, k))

            for g in range(2):
                unit(g, g, 0)
            split_ab(0, 0, 0)
            unit(2, 0, 1)
            split_ab(1, 1, 0)
            turns(pool, turn)
            x1_low(GROUPS - 2, 0, GROUPS // 2 - 1)
            residual(GROUPS - 1, 1, GROUPS // 2 - 1)
            x1_low(GROUPS - 1, 1, GROUPS // 2 - 1)

            pool.wait_ge(S["gates"], 4 * (3 * H // 4 + 1))
            pool.memset(x1r[32:HALF], 0.0).then_inc(S["x1r_pads"], 1)

        @block.vector
        def _(dve):
            dve.wait_ge(S["consts0"], 48)
            dve.tensor_tensor(t1[:, 0:1], col1_sb[:, 0:1], col1_sb[:, 1:2], ALU.mult).then_inc(S["t1_ready"], 1)
            dve.wait_ge(S["t1_ready"], 1)
            dve.tensor_tensor(t1[:, 1:2], t1[:, 0:1], col1_sb[:, 2:3], ALU.add).then_inc(S["t1_ready"], 1)

            def chunk(c, b, n):
                dve.wait_ge(S["y_ready"], c + 1)
                dve.tensor_copy(y3[:, b, 1], y3[:, b, 0].bitcast(F32)).then_inc(S["y_hi_ready"], 1)
                dve.wait_ge(S["y_hi_ready"], c + 1)
                dve.tensor_tensor(y3[:, b, 2], y3[:, b, 0].bitcast(F32), y3[:, b, 1].bitcast(F32), ALU.subtract) \
                    .then_inc(S["y_split"], 1)

            chunks(dve, chunk)
            dve.wait_ge(S["nrm_ready"], 1)
            dve.tensor_scalar(nmax[:], nrm[:], 1e-12, None, ALU.max).then_inc(S["norm_parts"], 1)
            dve.tensor_scalar(nunit[:], nrm[:], 1e12, 1.0, ALU.mult, ALU.min).then_inc(S["norm_parts"], 1)
            dve.wait_ge(S["norm_parts"], 2)
            dve.reciprocal(nrows[:, 0], nmax[:]).then_inc(S["nrows_ready"], 1)
            dve.tensor_scalar(nrows[:, 1], nmax[:], -0.5, None, ALU.mult).then_inc(S["nrows_ready"], 1)
            dve.tensor_tensor(nrows[:, 2], nunit[:], nunit[:], ALU.mult).then_inc(S["nrows_ready"], 1)

            dve.wait_ge(S["consts1"], 6 * 16)
            EP = S["edge_parts"]
            dve.tensor_tensor(we[:, 0], we_raw[:, 0], we_raw[:, 1], ALU.subtract).then_inc(EP, 1)
            dve.tensor_tensor(we[:, 1], we_raw[:, 1], we_mul[:], ALU.mult).then_inc(EP, 1)
            dve.tensor_tensor(t2[HALF:TOP, 0:1], col2_sb[HALF:TOP, 0:1], col2_sb[HALF:TOP, 1:2], ALU.mult) \
                .then_inc(EP, 1)
            dve.wait_ge(EP, 3)
            dve.tensor_tensor(we[:, 0], we[:, 0], we_mul[:], ALU.mult).then_inc(EP, 1)
            dve.tensor_tensor(t2[HALF:TOP, 1:2], t2[HALF:TOP, 0:1], col2_sb[HALF:TOP, 2:3], ALU.add) \
                .then_inc(EP, 1)
            dve.wait_ge(EP, 5)
            dve.tensor_tensor(we[:], we[:], we_add[:], ALU.add).then_inc(EP, 1)
            dve.wait_ge(EP, 6)
            dve.tensor_copy(we_hi[:], we[:]).then_inc(S["edge_w"], 1)
            dve.wait_ge(S["edge_w"], 1)
            dve.tensor_tensor(we_lo[:], we[:], we_hi[:].bitcast(F32), ALU.subtract).then_inc(S["edge_w"], 1)

            dve.wait_ge(S["own_loaded"], 16)
            for k in range(WIN):
                dve.tensor_copy(onehot[HALF:P, k // 4, k % 4], ab[HALF:P].rearrange("p w n -> p (w n)")[:, 0:E9]) \
                    .then_inc(S["own_set"], 1)

            TP = S["topk_parts"]
            keys_of = [p_keys[:, NODES * t:NODES * t + NODES] for t in range(4)]

            def topk(g, b, n, part):
                if part == 0:
                    dve.wait_ge(S["keys_done"], g + 1)
                    passed(dve, "dve_passed")
                    for t in range(4):
                        ins = dve.max(val8[:, t, 0:8], keys_of[t])
                    ins.then_inc(TP, 1)
                    return
                dve.wait_ge(TP, g * 3 + part)
                if part == 1 and later(n):
                    dve.wait_ge(S[f"idx_stored{b}"], n * 16)
                passed(dve, "dve_passed")
                for t in range(4):
                    if part == 1:
                        dve.max_index(idx[:, b, t, 0:8], val8[:, t, 0:8], keys_of[t])
                        ins = dve.match_replace(keys2[:, t], val8[:, t, 0:8], keys_of[t], LOWEST)
                    elif part == 2:
                        ins = dve.max(val8[:, t, 8:16], keys2[:, t])
                    else:
                        ins = dve.max_index(idx[:, b, t, 8:16], val8[:, t, 8:16], keys2[:, t])
                ins.then_inc(S["topk_done"] if part == 3 else TP, 1)

            def one_hot(g, b, n, half):
                if half == 0:
                    dve.wait_ge(S[f"idx_here{b}"], n * 16 + 16)
                if later(g):
                    dve.wait_ge(S["z_done"], g * 8 + (4 * half - 4))
                at = HALF * b
                dve.tensor_scalar(onehot[0:HALF, half], ib[at:at + HALF, 4 * half:4 * half + 4],
                                  jcol_sb[at:at + HALF, 0:1], None, ALU.is_equal).then_inc(S["onehots"], 1)

            def maxima(g, b, n, q):
                dve.wait_ge(S["gelus"], g * 8 + (2 * q + 2))
                if q == 0 and later(g, 2):
                    dve.wait_ge(S["fc2_done"], g - 1)
                at = HG * (q // 2) + 2 * WS * (q % 2)
                dst = hmax[:, b, HG * (q // 2):HG * (q // 2) + HG] \
                    .rearrange("p (r w c) -> p w r c", r=WS, c=WS)[:, 2 * (q % 2):2 * (q % 2) + 2]
                dve.tensor_reduce(dst, gel[:, q % 2].rearrange("p w (r c k) -> p w r c k", r=WS, k=K),
                                  AX_X, ALU.max).then_inc(S["maxed"], 1)

            def scan_weights(part):
                if part == 0:
                    dve.wait_ge(S["wl_loaded"], 16)
                    n = 0
                    for aps in ([wl_raw[:, d, 0] for d in range(2)],
                                [wl_raw[:, d, 1, :, HALF:TOP] for d in range(2)],
                                [wl_raw[0:C, d] for d in range(2)]):
                        for ap in aps:
                            dve.tensor_scalar(ap, ap, 0.5, None, ALU.mult).then_inc(S["wl_scaled"], 1)
                            n += 1
                        dve.wait_ge(S["wl_scaled"], n)
                elif part == 1:
                    dve.tensor_copy(wl_hi[:], wl_raw[:]).then_inc(S["wl_split"], 1)
                else:
                    dve.wait_ge(S["wl_split"], 1)
                    dve.tensor_tensor(wl_lo[:], wl_raw[:], wl_hi[:].bitcast(F32), ALU.subtract) \
                        .then_inc(S["wl_split"], 1)

            def turn(j, b):
                now, next_ = nth(j, b, 0), nth(j, b, 1)
                last = not exists(next_[0])

                def find(part):
                    if exists(nth(j, b, 2)[0]):
                        topk(*nth(j, b, 2), part)

                find(0)
                one_hot(*now, 1)
                find(1)
                maxima(*now, 0)
                find(2)
                maxima(*now, 1)
                maxima(*now, 2)
                find(3)
                if exists(next_[0]):
                    one_hot(*next_, 0)
                maxima(*now, 3)
                if last:
                    for part in range(3):
                        scan_weights(part)

            for g in range(2):
                for part in range(4):
                    topk(g, g, 0, part)
            one_hot(0, 0, 0, 0)
            turns(dve, turn)

            for b in range(2):
                dve.wait_ge(S[f"x1_stored{b}"], 32 * (GROUPS // 2))
            dve.wait_ge(S["x1_split"], GROUPS)
            for t in (ti, tf, tg, c2):
                dve.memset(t[:], 0.0).then_inc(S["scan_init"], 1)
            dve.wait_ge(S["scan_init"], 4)

            def cell(s, x, last=False):
                dve.wait_ge(S["tanh_if"], s * 8 + (4 * x + 4))
                if later(s):
                    dve.wait_ge(S["cells"], s * 2 + (x - 1))
                dve.scalar_tensor_tensor(cu[0:TOP, x], tf[0:TOP, x], 1.0, c2[0:TOP, x], ALU.add, ALU.mult)
                dve.wait_ge(S["tanh_go"], s * 8 + (4 * x + 2))
                dve.scalar_tensor_tensor(cv[0:TOP, x], ti[0:TOP, x], 1.0, tg[0:TOP, x], ALU.add, ALU.mult) \
                    .then_inc(S["cell_parts"], 1)
                dve.wait_ge(S["cell_parts"], s * 2 + (x + 1))
                dve.scalar_tensor_tensor(c2[0:TOP, x], cu[0:TOP, x], 0.5, cv[0:TOP, x], ALU.mult, ALU.add) \
                    .then_inc(S["cells"], 1)
                dve.wait_ge(S["tanh_c"], s * 2 + (x + 1))
                if later(s):
                    dve.wait_ge(S[f"hist{x}"], s * 32)
                for d in range(2):
                    at = HALF * d
                    dve.scalar_tensor_tensor(h2[:, x, d], to[at:at + C, x], 1.0, tc[at:at + C, x],
                                             ALU.add, ALU.mult).then_inc(S["h2_ready"], 1)
                if last:
                    return
                for d, row in ((0, s + 1), (1, s * -1 + (H - 2))):
                    dve.wait_ge(S["h_hi"], s * 4 + (2 * x + d + 1))
                    dve.tensor_tensor(h_rows(xh_lo, row, x), h2[:, x, d].rearrange("p (b w) -> p b w", w=W),
                                      h_rows(xh_hi, row, x).bitcast(F32), ALU.subtract).then_inc(S["h_lo"], 1)

            def stats(i):
                dve.wait_ge(S["y_kept"], i + 1)
                dve.bn_stats(one_row(bst, i), one_row(y_sb, i)).then_inc(S["y_stats"], 1)

            def step(s, projects=False):
                for x in range(2):
                    cell(s, x, last=isinstance(s, int) and s == H - 1)
                    if x == 1 and projects:
                        stats(s - (H // 2 + 3))

            step(0)
            with dve.Fori(0, H // 4) as j:
                for b in range(2):
                    step(j * 2 + (1 + b))
            dve.wait_ge(S["consts2"], 48)
            dve.tensor_scalar(wp_sb[:], wp_sb[:], 0.5, None, ALU.mult).then_inc(S["wp_ready"], 1)
            step(17)
            step(18)
            step(19, projects=True)
            with dve.Fori(1, H // 4 - 2) as j:
                for b in range(2):
                    step(j * 2 + (18 + b), projects=True)
            step(30, projects=True)
            step(31, projects=True)
            for i in range(13, H // 2):
                stats(i)
            dve.wait_ge(S["y_stats"], H // 2)
            dve.bn_aggr(mv[:, :], bst[:].rearrange("p r n -> p (r n)")).then_inc(S["fold"], 1)
            dve.wait_ge(S["comb_mm"], 1)
            ST = S["stat"]
            dve.tensor_copy(st[:, 0:1], p_comb[:, 4:5]).then_inc(ST, 1)
            dve.wait_ge(ST, 1)
            dve.scalar_tensor_tensor(st[:, 1:2], st[:, 0:1], st[:, 0:1], p_comb[:, 1:2], ALU.mult, ALU.add) \
                .then_inc(ST, 1)
            dve.wait_ge(ST, 2)
            dve.tensor_scalar(st[:, 2:3], st[:, 1:2], EPS, None, ALU.add).then_inc(ST, 1)
            dve.wait_ge(ST, 4)
            dve.reciprocal(st[:, 4:5], st[:, 3:4]).then_inc(ST, 1)
            dve.wait_ge(ST, 5)
            dve.tensor_tensor(st[:, 5:6], st[:, 4:5], gb_sb[:, 0:1], ALU.mult).then_inc(ST, 1)
            dve.wait_ge(ST, 6)
            dve.tensor_tensor(st[:, 6:7], st[:, 5:6], p_comb[:, 0:1], ALU.mult).then_inc(ST, 1)
            dve.wait_ge(ST, 7)
            dve.tensor_tensor(st[:, 7:8], gb_sb[:, 1:2], st[:, 6:7], ALU.subtract).then_inc(ST, 1)

            dve.wait_ge(S["x1r_loaded"], 16 * (H // 2 + 4))
            with dve.Fori(0, H // 4) as j:
                dve.wait_ge(S["relus"], j * 2 + 2)
                for k in range(2):
                    row = one_row(y_sb, j * 2 + k)[0:TOP]
                    dve.tensor_tensor(row, row, one_row(x1r, j * 2 + k)[0:TOP], ALU.add).then_inc(S["summed"], 1)


def kernel(**inputs):
    import numpy as np
    import concourse.bacc as bacc
    from concourse.bass_utils import run_bass_kernel_spmd

    f = {k: np.asarray(v) for k, v in inputs.items()}
    z = np.zeros

    def halves(cols):
        t = z((P, cols.shape[1]), np.float32)
        t[0:C] = t[HALF:TOP] = cols
        return t

    x = f["x"].reshape(2, PAIRS, C, WROWS, WS, W // WS, WS)
    xs = z((TOP, CHUNKS, CHUNK), np.float32)
    by_window = x.transpose(0, 2, 3, 1, 5, 4, 6).reshape(2, C, CHUNKS, CHUNK)
    xs[0:C], xs[HALF:TOP] = by_window[0], by_window[1]
    xrow = x.transpose(2, 3, 1, 0, 4, 5, 6).reshape(C, GROUPS, GN)
    w1 = z((P, P), np.float32)
    w1[0:C, 0:C] = w1[HALF:TOP, HALF:TOP] = f["L0_conv_fc1_w"].T
    ones_sel = z((P, CHUNKS, 2 * CHUNKS), np.float32)
    for c in range(CHUNKS):
        ones_sel[0:C, c, 2 * c] = ones_sel[HALF:TOP, c, 2 * c + 1] = 1.0
    col1 = halves(np.stack([f["L0_conv_fc1_b"], f["L0_conv_fc1_s"], f["L0_conv_fc1_t"]], 1))
    col2 = halves(np.stack([f["L0_conv_fc2_b"], f["L0_conv_fc2_s"], f["L0_conv_fc2_t"]], 1))
    jcol = (np.arange(P, dtype=np.float32) % NODES).reshape(P, 1)
    ewt = f["L0_conv_ew"].T.reshape(2, C, O)
    wedge = z((P, 2, O), np.float32)
    wedge[0:C] = wedge[HALF:TOP] = ewt.transpose(1, 0, 2)
    wedge[TOP, 0] = f["L0_conv_eb"]
    edge_shift = z((P, 2, O), np.float32)
    edge_shift[TOP, 0] = f["L0_conv_et"]
    ident9 = np.repeat(np.eye(NODES, dtype=np.float32), K, axis=1)
    w2 = np.ascontiguousarray(f["L0_conv_fc2_w"].T)
    wl = z((P, 2, 2, TAPS, TOP), np.float32)
    for d, (wn, bn) in enumerate((("L1_conv_w_f", "L1_conv_b_f"), ("L1_conv_w_b", "L1_conv_b_b"))):
        mid = f[wn][:, :, 1, :].reshape(4, C, 2, C, TAPS)
        for gate in range(4):
            m, at = gate // 2, HALF * (gate % 2)
            t = mid[gate].transpose(1, 2, 3, 0)
            wl[HALF:TOP, d, m, :, at:at + C] = t[0]
            wl[0:C, d, m, :, at:at + C] = t[1]
            wl[C, d, m, 1, at:at + C] = f[bn].reshape(4, C)[gate]
    wp = z((O, HALF), np.float32)
    wp[:, 0:C] = f["L1_conv_w_proj"].T
    gb = halves(np.stack([f["L1_conv_gamma"], f["L1_conv_beta"]], 1))
    comb = z((P, 2, P), np.float32)
    for c in range(HALF):
        for q in range(2):
            for r in range(2):
                comb[HALF * q + c, 0, HALF * r + c] = 0.5
                comb[HALF * q + c, 1, HALF * r + c] = 0.5 - q

    arrays = dict(xs=xs, xrow=xrow, w1=w1, ones_sel=ones_sel, col1=col1, jcol=jcol, wedge=wedge,
                  edge_scale=f["L0_conv_es"], edge_shift=edge_shift, ident9=ident9, w2=w2, col2=col2,
                  wl=wl, wp=wp, gb=gb, comb=comb)
    arrays = {k: np.ascontiguousarray(v) for k, v in arrays.items()}
    nc = bacc.Bacc("TRN2", target_bir_lowering=False, num_devices=1)
    aps = {k: nc.dram_tensor(k, v.shape, F32, kind="ExternalInput").ap()
           for k, v in arrays.items()}
    out = nc.dram_tensor("out", (2, C, H // 2, B * W), F32, kind="ExternalOutput").ap()
    build(nc, **aps, out=out)
    r = run_bass_kernel_spmd(nc, [arrays], core_ids=[0])
    lower, upper = r.results[0]["out"].reshape(2, C, H // 2, B, W)
    return np.concatenate([upper[:, ::-1], lower], 1).transpose(2, 0, 1, 3)
```
